# Optimizing a Trainium2 kernel written in Bass

```python
import numpy as np
import jax
import jax.numpy as jnp

def _softmax(x, axis=-1):
    return jax.nn.softmax(x, axis=axis)

def _gelu(x):
    return jax.nn.gelu(x, approximate=True)

def _silu(x):
    return jax.nn.silu(x)

def _sigmoid(x):
    return jax.nn.sigmoid(x)

def _layernorm(x, axis=-1, eps=1e-05):
    m = jnp.mean(x, axis=axis, keepdims=True)
    v = jnp.var(x, axis=axis, keepdims=True)
    return (x - m) / jnp.sqrt(v + eps)

def _scatter_add(tgt, idx, src, axis=0):
    return tgt.at[idx].add(src)

def _segment_sum(src, seg, n):
    return jax.ops.segment_sum(src, seg, n)
kernel_name = 'mk_gnn_ffn_d4_gnn_r32_d01007'

def setup_inputs(seed: int=0):
    np.random.seed(seed)
    _w = jnp.asarray

    def _rec_inputs():
        import jax
        import jax.numpy as jnp
        _gk = jax.random.key(seed)
        x = 3.789e-05 + 1 * jax.random.normal(jax.random.fold_in(_gk, 1), (3125, 256), jnp.float32)
        src = jax.random.randint(jax.random.fold_in(_gk, 2), (50000,), 0, 3125, jnp.int32)
        dst = jnp.minimum((3125 * jax.random.uniform(jax.random.fold_in(_gk, 3), (50000,)) ** 2.0).astype(jnp.int32), 99999)
        _o = jnp.argsort(dst, stable=True)
        src = src[_o]
        dst = dst[_o]
        edge_attr3_1x1 = jax.random.uniform(jax.random.fold_in(_gk, 12), (50000, 1, 1), jnp.float32, 0.0, 0.999998)
        edge_attr_2 = -0.000414295 + 0.999828 * jax.random.normal(jax.random.fold_in(_gk, 13), (50000, 2), jnp.float32)
        edge_weight = jax.random.uniform(jax.random.fold_in(_gk, 15), (50000,), jnp.float32, 0.0, 0.999998)
        node_vec1 = jax.random.uniform(jax.random.fold_in(_gk, 16), (3125, 1), jnp.float32, 0.0, 0.999957)
        return (x, src, dst, edge_attr3_1x1, edge_attr_2, edge_weight, node_vec1)
    x, src, dst, edge_attr3_1x1, edge_attr_2, edge_weight, node_vec1 = _rec_inputs()

    def _L0_gnn_setup():
        import jax, jax.numpy as jnp
        import numpy as np
        N, F_IN, H, OUT, E = (1000, 256, 4, 64, 16000)
        NEG_SLOPE = 0.2
        key = jax.random.key(seed)
        ks = jax.random.split(key, 7)
        return {'feat': jax.random.normal(ks[0], (N, F_IN), dtype=jnp.float32), 'dist': jax.random.uniform(ks[1], (E, 1, 1), dtype=jnp.float32), 'W': jax.random.normal(ks[2], (F_IN, H * OUT), dtype=jnp.float32) * (1.0 / np.sqrt(F_IN)), 'w_att_src': jax.random.normal(ks[3], (1, H, OUT), dtype=jnp.float32) * 0.1, 'w_att_dst': jax.random.normal(ks[4], (1, H, OUT), dtype=jnp.float32) * 0.1, 'src': jax.random.randint(ks[5], (E,), 0, N, dtype=jnp.int32), 'dst': jax.random.randint(ks[6], (E,), 0, N, dtype=jnp.int32)}
    _L0_gnn_all = _L0_gnn_setup()
    _L0_gnn_in = {k: v for k, v in _L0_gnn_all.items() if k in ('W', 'w_att_src', 'w_att_dst')}
    del _L0_gnn_all

    def _L0_ffn_setup():
        import jax, jax.numpy as jnp
        import numpy as np
        B, S, H, F, E, K = (8, 128, 256, 512, 16, 2)
        EPS = 1e-05
        key = jax.random.key(seed)
        ks = jax.random.split(key, 9)
        sc = 0.02
        return {'x': jax.random.normal(ks[0], (B, S, H), dtype=jnp.float32), 'gate_w': jax.random.normal(ks[1], (H, E), dtype=jnp.float32) * sc, 'gate_b': jnp.zeros((E,), dtype=jnp.float32), 'w1': jax.random.normal(ks[2], (E, H, F), dtype=jnp.float32) * sc, 'b1': jnp.zeros((E, F), dtype=jnp.float32), 'w2': jax.random.normal(ks[3], (E, F, H), dtype=jnp.float32) * sc, 'b2': jnp.zeros((E, H), dtype=jnp.float32), 'gamma': jnp.ones((H,), dtype=jnp.float32), 'beta': jnp.zeros((H,), dtype=jnp.float32)}
    _L0_ffn_all = _L0_ffn_setup()
    _L0_ffn_in = {k: v for k, v in _L0_ffn_all.items() if k in ('gate_w', 'gate_b', 'w1', 'b1', 'w2', 'b2', 'gamma', 'beta')}
    del _L0_ffn_all

    def _L1_gnn_setup():
        import jax, jax.numpy as jnp
        import numpy as np
        N = 50000
        E = 25000
        NFEAT = 256
        NHID = 64
        NHEADS = 4
        NOUT = 256
        NEG_SLOPE = 0.2
        BN_EPS = 1e-05
        LN_EPS = 1e-05

        def _gat_conv(x, edge_index, W, att_src, att_dst, bias, concat):
            n = x.shape[0]
            H, C = att_src.shape
            xp = (x @ W).reshape(n, H, C)
            loop = jnp.arange(n, dtype=edge_index.dtype)
            src = jnp.concatenate([edge_index[0], loop])
            dst = jnp.concatenate([edge_index[1], loop])
            a_src = jnp.einsum('nhc,hc->nh', xp, att_src)
            a_dst = jnp.einsum('nhc,hc->nh', xp, att_dst)
            e = jax.nn.leaky_relu(a_src[src] + a_dst[dst], NEG_SLOPE)
            m = jax.ops.segment_max(e, dst, num_segments=n)
            e = jnp.exp(e - m[dst])
            denom = jax.ops.segment_sum(e, dst, num_segments=n)
            alpha = e / (denom[dst] + 1e-16)
            out = jax.ops.segment_sum(alpha[:, :, None] * xp[src], dst, num_segments=n)
            out = out.reshape(n, H * C) if concat else out.mean(axis=1)
            return out + bias
        key = jax.random.key(seed)
        ks = jax.random.split(key, 12)
        g = lambda k, s: jax.random.normal(k, s, dtype=jnp.float32) * 0.05
        inp = {'x': jax.random.normal(ks[0], (N, NFEAT), dtype=jnp.float32), 'edge_index': jax.random.randint(ks[1], (2, E), 0, N, dtype=jnp.int32), 'W1': g(ks[2], (NFEAT, NHEADS * NHID)), 'att_src1': g(ks[3], (NHEADS, NHID)), 'att_dst1': g(ks[4], (NHEADS, NHID)), 'bias1': jnp.zeros((NHEADS * NHID,), jnp.float32), 'W2': g(ks[5], (NHEADS * NHID, NOUT)), 'att_src2': g(ks[6], (1, NOUT)), 'att_dst2': g(ks[7], (1, NOUT)), 'bias2': jnp.zeros((NOUT,), jnp.float32), 'bn_gamma': jnp.ones((NOUT,), jnp.float32), 'bn_beta': jnp.zeros((NOUT,), jnp.float32), 'bn_mean': g(ks[8], (NOUT,)), 'bn_var': jnp.ones((NOUT,), jnp.float32), 'ln_gamma': jnp.ones((NOUT,), jnp.float32), 'ln_beta': jnp.zeros((NOUT,), jnp.float32)}
        return inp
    _L1_gnn_all = _L1_gnn_setup()
    _L1_gnn_in = {k: v for k, v in _L1_gnn_all.items() if k in ('W1', 'att_src1', 'att_dst1', 'bias1', 'W2', 'att_src2', 'att_dst2', 'bias2', 'bn_gamma', 'bn_beta', 'bn_mean', 'bn_var', 'ln_gamma', 'ln_beta')}
    del _L1_gnn_all

    def _L1_ffn_setup():
        import jax, jax.numpy as jnp
        import numpy as np
        BN_EPS = 0.001

        def _bn(h, g, b, m, v):
            return g * (h - m) * jax.lax.rsqrt(v + BN_EPS) + b
        key = jax.random.key(seed)
        ks = jax.random.split(key, 8)
        B, F, Df = (256, 64, 256)
        E, H, D = (8, 256, 256)
        s1 = 1.0 / np.sqrt(Df)
        s2 = 1.0 / np.sqrt(H)
        return {'x': jax.random.normal(ks[0], (B, F, Df), jnp.float32), 'Wr': jax.random.normal(ks[1], (Df, E), jnp.float32) * s1, 'br': jnp.zeros((E,), jnp.float32), 'W1': jax.random.normal(ks[2], (E, Df, H), jnp.float32) * s1, 'b1': jnp.zeros((E, H), jnp.float32), 'g1': jnp.ones((E, H), jnp.float32), 'be1': jnp.zeros((E, H), jnp.float32), 'm1': jnp.zeros((E, H), jnp.float32), 'v1': jnp.ones((E, H), jnp.float32), 'W2': jax.random.normal(ks[3], (E, H, H), jnp.float32) * s2, 'b2': jnp.zeros((E, H), jnp.float32), 'g2': jnp.ones((E, H), jnp.float32), 'be2': jnp.zeros((E, H), jnp.float32), 'm2': jnp.zeros((E, H), jnp.float32), 'v2': jnp.ones((E, H), jnp.float32), 'Wo': jax.random.normal(ks[4], (E, H, D), jnp.float32) * s2, 'bo': jnp.zeros((E, D), jnp.float32)}
    _L1_ffn_all = _L1_ffn_setup()
    _L1_ffn_in = {k: v for k, v in _L1_ffn_all.items() if k in ('Wr', 'br', 'W1', 'b1', 'g1', 'be1', 'm1', 'v1', 'W2', 'b2', 'g2', 'be2', 'm2', 'v2', 'Wo', 'bo')}
    del _L1_ffn_all

    def _L2_gnn_setup():
        import jax, jax.numpy as jnp
        import numpy as np
        N_NODES = 50000
        N_EDGES = 25000
        D = 256
        EPS = 1e-08
        BN_EPS = 1e-05
        key = jax.random.key(seed)
        ks = jax.random.split(key, 11)
        return {'h': jax.random.normal(ks[0], (N_NODES, D), jnp.float32), 'eig': jax.random.normal(ks[1], (N_EDGES, 2), jnp.float32), 'snorm_n': jax.random.uniform(ks[2], (N_NODES, 1), jnp.float32), 'W1': jax.random.normal(ks[3], (2 * D, D), jnp.float32) * (1.0 / np.sqrt(2 * D)), 'b1': jnp.zeros((D,), jnp.float32), 'W2': jax.random.normal(ks[4], (4 * D, D), jnp.float32) * (1.0 / np.sqrt(4 * D)), 'b2': jnp.zeros((D,), jnp.float32), 'gamma': jnp.ones((D,), jnp.float32), 'beta': jnp.zeros((D,), jnp.float32), 'src': jax.random.randint(ks[5], (N_EDGES,), 0, N_NODES, jnp.int64 if jax.config.jax_enable_x64 else jnp.int32), 'dst': jax.random.randint(ks[6], (N_EDGES,), 0, N_NODES, jnp.int64 if jax.config.jax_enable_x64 else jnp.int32)}
    _L2_gnn_all = _L2_gnn_setup()
    _L2_gnn_in = {k: v for k, v in _L2_gnn_all.items() if k in ('W1', 'b1', 'W2', 'b2', 'gamma', 'beta')}
    del _L2_gnn_all

    def _L2_ffn_setup():
        import jax, jax.numpy as jnp
        import numpy as np
        DIM = 256
        H = 8
        D = 64
        G = 64
        INNER = H * D
        SCALE = D ** (-0.5)
        key = jax.random.key(seed)
        ks = jax.random.split(key, 12)
        B, N = (4, 512)
        x = jax.random.normal(ks[0], (B, N, DIM), dtype=jnp.float32)
        s = lambda fan_in: 1.0 / np.sqrt(fan_in)
        W_fx = jax.random.normal(ks[1], (DIM, INNER), dtype=jnp.float32) * s(DIM)
        b_fx = jnp.zeros((INNER,), dtype=jnp.float32)
        W_x = jax.random.normal(ks[2], (DIM, INNER), dtype=jnp.float32) * s(DIM)
        b_x = jnp.zeros((INNER,), dtype=jnp.float32)
        A = jax.random.normal(ks[3], (G, D), dtype=jnp.float32)
        Q, _ = jnp.linalg.qr(A.T)
        W_slice = Q[:, :G].astype(jnp.float32)
        b_slice = jnp.zeros((G,), dtype=jnp.float32)
        W_q = jax.random.normal(ks[4], (D, D), dtype=jnp.float32) * s(D)
        W_k = jax.random.normal(ks[5], (D, D), dtype=jnp.float32) * s(D)
        W_v = jax.random.normal(ks[6], (D, D), dtype=jnp.float32) * s(D)
        W_out = jax.random.normal(ks[7], (INNER, DIM), dtype=jnp.float32) * s(INNER)
        b_out = jnp.zeros((DIM,), dtype=jnp.float32)
        temperature = jnp.ones((1, H, 1, 1), dtype=jnp.float32) * 0.5
        return {'x': x, 'W_fx': W_fx, 'b_fx': b_fx, 'W_x': W_x, 'b_x': b_x, 'W_slice': W_slice, 'b_slice': b_slice, 'W_q': W_q, 'W_k': W_k, 'W_v': W_v, 'W_out': W_out, 'b_out': b_out, 'temperature': temperature}
    _L2_ffn_all = _L2_ffn_setup()
    _L2_ffn_in = {k: v for k, v in _L2_ffn_all.items() if k in ('W_fx', 'b_fx', 'W_x', 'b_x', 'W_slice', 'b_slice', 'W_q', 'W_k', 'W_v', 'W_out', 'b_out', 'temperature')}
    del _L2_ffn_all

    def _L3_gnn_setup():
        import jax, jax.numpy as jnp
        import numpy as np
        N, E, D, H, C = (625, 10000, 256, 8, 32)
        NEG_SLOPE = 0.2
        key = jax.random.key(seed)
        ks = jax.random.split(key, 9)
        s = 1.0 / np.sqrt(D)
        x = jax.random.normal(ks[0], (N, D), dtype=jnp.float32)
        edge_index = jax.random.randint(ks[1], (2, E), 0, N, dtype=jnp.int32)
        edge_attr = jax.random.uniform(ks[2], (E,), dtype=jnp.float32, minval=0.05, maxval=1.0)
        W_l = jax.random.normal(ks[3], (D, H * C), dtype=jnp.float32) * s
        b_l = jax.random.normal(ks[4], (H * C,), dtype=jnp.float32) * 0.01
        W_r = jax.random.normal(ks[5], (D, H * C), dtype=jnp.float32) * s
        b_r = jax.random.normal(ks[6], (H * C,), dtype=jnp.float32) * 0.01
        att = jax.random.normal(ks[7], (H, C), dtype=jnp.float32) * (1.0 / np.sqrt(C))
        bias = jax.random.normal(ks[8], (H * C,), dtype=jnp.float32) * 0.01
        return {'x': x, 'edge_index': edge_index, 'edge_attr': edge_attr, 'W_l': W_l, 'b_l': b_l, 'W_r': W_r, 'b_r': b_r, 'att': att, 'bias': bias}
    _L3_gnn_all = _L3_gnn_setup()
    _L3_gnn_in = {k: v for k, v in _L3_gnn_all.items() if k in ('W_l', 'b_l', 'W_r', 'b_r', 'att', 'bias')}
    del _L3_gnn_all

    def _L3_ffn_setup():
        import jax, jax.numpy as jnp
        import numpy as np
        E, D, H, TOP_K = (6, 256, 256, 2)
        ROUTER_H = D // 2
        key = jax.random.key(seed)
        ks = jax.random.split(key, 12)
        s = 1.0 / np.sqrt(D)
        sh = 1.0 / np.sqrt(H)
        sr = 1.0 / np.sqrt(ROUTER_H)
        return {'features': jax.random.normal(ks[0], (8, 128, D), dtype=jnp.float32), 'router_w1': jax.random.uniform(ks[1], (D, ROUTER_H), jnp.float32, -s, s), 'router_b1': jnp.zeros((ROUTER_H,), jnp.float32), 'router_w2': jax.random.uniform(ks[2], (ROUTER_H, E), jnp.float32, -sr, sr), 'router_b2': jnp.zeros((E,), jnp.float32), 'expert_w1': jax.random.uniform(ks[3], (E, D, H), jnp.float32, -s, s), 'expert_b1': jnp.zeros((E, H), jnp.float32), 'expert_w2': jax.random.uniform(ks[4], (E, H, H), jnp.float32, -sh, sh), 'expert_b2': jnp.zeros((E, H), jnp.float32), 'expert_w3': jax.random.uniform(ks[5], (E, H, D), jnp.float32, -sh, sh), 'expert_b3': jnp.zeros((E, D), jnp.float32)}
    _L3_ffn_all = _L3_ffn_setup()
    _L3_ffn_in = {k: v for k, v in _L3_ffn_all.items() if k in ('router_w1', 'router_b1', 'router_w2', 'router_b2', 'expert_w1', 'expert_b1', 'expert_w2', 'expert_b2', 'expert_w3', 'expert_b3')}
    del _L3_ffn_all
    return {'x': x, 'src': src, 'dst': dst, 'edge_attr3_1x1': edge_attr3_1x1, 'edge_attr_2': edge_attr_2, 'edge_weight': edge_weight, 'node_vec1': node_vec1, 'L0_gnn_W': _L0_gnn_in['W'], 'L0_gnn_w_att_src': _L0_gnn_in['w_att_src'], 'L0_gnn_w_att_dst': _L0_gnn_in['w_att_dst'], 'L0_ffn_gate_w': _L0_ffn_in['gate_w'], 'L0_ffn_gate_b': _L0_ffn_in['gate_b'], 'L0_ffn_w1': _L0_ffn_in['w1'], 'L0_ffn_b1': _L0_ffn_in['b1'], 'L0_ffn_w2': _L0_ffn_in['w2'], 'L0_ffn_b2': _L0_ffn_in['b2'], 'L0_ffn_gamma': _L0_ffn_in['gamma'], 'L0_ffn_beta': _L0_ffn_in['beta'], 'L1_gnn_W1': _L1_gnn_in['W1'], 'L1_gnn_att_src1': _L1_gnn_in['att_src1'], 'L1_gnn_att_dst1': _L1_gnn_in['att_dst1'], 'L1_gnn_bias1': _L1_gnn_in['bias1'], 'L1_gnn_W2': _L1_gnn_in['W2'], 'L1_gnn_att_src2': _L1_gnn_in['att_src2'], 'L1_gnn_att_dst2': _L1_gnn_in['att_dst2'], 'L1_gnn_bias2': _L1_gnn_in['bias2'], 'L1_gnn_bn_gamma': _L1_gnn_in['bn_gamma'], 'L1_gnn_bn_beta': _L1_gnn_in['bn_beta'], 'L1_gnn_bn_mean': _L1_gnn_in['bn_mean'], 'L1_gnn_bn_var': _L1_gnn_in['bn_var'], 'L1_gnn_ln_gamma': _L1_gnn_in['ln_gamma'], 'L1_gnn_ln_beta': _L1_gnn_in['ln_beta'], 'L1_ffn_Wr': _L1_ffn_in['Wr'], 'L1_ffn_br': _L1_ffn_in['br'], 'L1_ffn_W1': _L1_ffn_in['W1'], 'L1_ffn_b1': _L1_ffn_in['b1'], 'L1_ffn_g1': _L1_ffn_in['g1'], 'L1_ffn_be1': _L1_ffn_in['be1'], 'L1_ffn_m1': _L1_ffn_in['m1'], 'L1_ffn_v1': _L1_ffn_in['v1'], 'L1_ffn_W2': _L1_ffn_in['W2'], 'L1_ffn_b2': _L1_ffn_in['b2'], 'L1_ffn_g2': _L1_ffn_in['g2'], 'L1_ffn_be2': _L1_ffn_in['be2'], 'L1_ffn_m2': _L1_ffn_in['m2'], 'L1_ffn_v2': _L1_ffn_in['v2'], 'L1_ffn_Wo': _L1_ffn_in['Wo'], 'L1_ffn_bo': _L1_ffn_in['bo'], 'L2_gnn_W1': _L2_gnn_in['W1'], 'L2_gnn_b1': _L2_gnn_in['b1'], 'L2_gnn_W2': _L2_gnn_in['W2'], 'L2_gnn_b2': _L2_gnn_in['b2'], 'L2_gnn_gamma': _L2_gnn_in['gamma'], 'L2_gnn_beta': _L2_gnn_in['beta'], 'L2_ffn_W_fx': _L2_ffn_in['W_fx'], 'L2_ffn_b_fx': _L2_ffn_in['b_fx'], 'L2_ffn_W_x': _L2_ffn_in['W_x'], 'L2_ffn_b_x': _L2_ffn_in['b_x'], 'L2_ffn_W_slice': _L2_ffn_in['W_slice'], 'L2_ffn_b_slice': _L2_ffn_in['b_slice'], 'L2_ffn_W_q': _L2_ffn_in['W_q'], 'L2_ffn_W_k': _L2_ffn_in['W_k'], 'L2_ffn_W_v': _L2_ffn_in['W_v'], 'L2_ffn_W_out': _L2_ffn_in['W_out'], 'L2_ffn_b_out': _L2_ffn_in['b_out'], 'L2_ffn_temperature': _L2_ffn_in['temperature'], 'L3_gnn_W_l': _L3_gnn_in['W_l'], 'L3_gnn_b_l': _L3_gnn_in['b_l'], 'L3_gnn_W_r': _L3_gnn_in['W_r'], 'L3_gnn_b_r': _L3_gnn_in['b_r'], 'L3_gnn_att': _L3_gnn_in['att'], 'L3_gnn_bias': _L3_gnn_in['bias'], 'L3_ffn_router_w1': _L3_ffn_in['router_w1'], 'L3_ffn_router_b1': _L3_ffn_in['router_b1'], 'L3_ffn_router_w2': _L3_ffn_in['router_w2'], 'L3_ffn_router_b2': _L3_ffn_in['router_b2'], 'L3_ffn_expert_w1': _L3_ffn_in['expert_w1'], 'L3_ffn_expert_b1': _L3_ffn_in['expert_b1'], 'L3_ffn_expert_w2': _L3_ffn_in['expert_w2'], 'L3_ffn_expert_b2': _L3_ffn_in['expert_b2'], 'L3_ffn_expert_w3': _L3_ffn_in['expert_w3'], 'L3_ffn_expert_b3': _L3_ffn_in['expert_b3']}

def reference(x, src, dst, edge_attr3_1x1, edge_attr_2, edge_weight, node_vec1, L0_gnn_W, L0_gnn_w_att_src, L0_gnn_w_att_dst, L0_ffn_gate_w, L0_ffn_gate_b, L0_ffn_w1, L0_ffn_b1, L0_ffn_w2, L0_ffn_b2, L0_ffn_gamma, L0_ffn_beta, L1_gnn_W1, L1_gnn_att_src1, L1_gnn_att_dst1, L1_gnn_bias1, L1_gnn_W2, L1_gnn_att_src2, L1_gnn_att_dst2, L1_gnn_bias2, L1_gnn_bn_gamma, L1_gnn_bn_beta, L1_gnn_bn_mean, L1_gnn_bn_var, L1_gnn_ln_gamma, L1_gnn_ln_beta, L1_ffn_Wr, L1_ffn_br, L1_ffn_W1, L1_ffn_b1, L1_ffn_g1, L1_ffn_be1, L1_ffn_m1, L1_ffn_v1, L1_ffn_W2, L1_ffn_b2, L1_ffn_g2, L1_ffn_be2, L1_ffn_m2, L1_ffn_v2, L1_ffn_Wo, L1_ffn_bo, L2_gnn_W1, L2_gnn_b1, L2_gnn_W2, L2_gnn_b2, L2_gnn_gamma, L2_gnn_beta, L2_ffn_W_fx, L2_ffn_b_fx, L2_ffn_W_x, L2_ffn_b_x, L2_ffn_W_slice, L2_ffn_b_slice, L2_ffn_W_q, L2_ffn_W_k, L2_ffn_W_v, L2_ffn_W_out, L2_ffn_b_out, L2_ffn_temperature, L3_gnn_W_l, L3_gnn_b_l, L3_gnn_W_r, L3_gnn_b_r, L3_gnn_att, L3_gnn_bias, L3_ffn_router_w1, L3_ffn_router_b1, L3_ffn_router_w2, L3_ffn_router_b2, L3_ffn_expert_w1, L3_ffn_expert_b1, L3_ffn_expert_w2, L3_ffn_expert_b2, L3_ffn_expert_w3, L3_ffn_expert_b3):
    import jax
    import jax.numpy as jnp

    def _L0_gnn_ref(feat, dist, W, w_att_src, w_att_dst, src, dst):
        import jax, jax.numpy as jnp
        import numpy as np
        N, F_IN, H, OUT, E = (1000, 256, 4, 64, 16000)
        NEG_SLOPE = 0.2
        n = feat.shape[0]
        ft = (feat @ W).reshape(n, H, OUT)
        e_src = jnp.sum(ft * w_att_src, axis=-1, keepdims=True)
        e_dst = jnp.sum(ft * w_att_dst, axis=-1, keepdims=True)
        e = e_src[src] + e_dst[dst]
        e = jnp.where(e >= 0, e, NEG_SLOPE * e)
        emax = jax.ops.segment_max(e, dst, num_segments=n)
        ex = jnp.exp(e - emax[dst])
        denom = jax.ops.segment_sum(ex, dst, num_segments=n)
        a = ex / denom[dst] * dist
        m = ft[src] * a
        out = jax.ops.segment_sum(m, dst, num_segments=n)
        return out.reshape(n, H * OUT)

    def _L0_ffn_ref(x, gate_w, gate_b, w1, b1, w2, b2, gamma, beta):
        import jax, jax.numpy as jnp
        import numpy as np
        B, S, H, F, E, K = (8, 128, 256, 512, 16, 2)
        EPS = 1e-05
        gate_logits = x @ gate_w + gate_b
        topk_vals, topk_idx = jax.lax.top_k(gate_logits, K)
        topk_w = jax.nn.softmax(topk_vals, axis=-1)
        h = jax.nn.relu(jnp.einsum('bsh,ehf->bsef', x, w1) + b1)
        expert_out = jnp.einsum('bsef,efh->bseh', h, w2) + b2
        sel = jnp.take_along_axis(expert_out, topk_idx[:, :, :, None], axis=2)
        moe = jnp.sum(topk_w[..., None] * sel, axis=2)
        y = x + moe
        mu = jnp.mean(y, axis=-1, keepdims=True)
        var = jnp.var(y, axis=-1, keepdims=True)
        return (y - mu) / jnp.sqrt(var + EPS) * gamma + beta

    def _L1_gnn_ref(x, edge_index, W1, att_src1, att_dst1, bias1, W2, att_src2, att_dst2, bias2, bn_gamma, bn_beta, bn_mean, bn_var, ln_gamma, ln_beta):
        import jax, jax.numpy as jnp
        import numpy as np
        N = 50000
        E = 25000
        NFEAT = 256
        NHID = 64
        NHEADS = 4
        NOUT = 256
        NEG_SLOPE = 0.2
        BN_EPS = 1e-05
        LN_EPS = 1e-05

        def _gat_conv(x, edge_index, W, att_src, att_dst, bias, concat):
            n = x.shape[0]
            H, C = att_src.shape
            xp = (x @ W).reshape(n, H, C)
            loop = jnp.arange(n, dtype=edge_index.dtype)
            src = jnp.concatenate([edge_index[0], loop])
            dst = jnp.concatenate([edge_index[1], loop])
            a_src = jnp.einsum('nhc,hc->nh', xp, att_src)
            a_dst = jnp.einsum('nhc,hc->nh', xp, att_dst)
            e = jax.nn.leaky_relu(a_src[src] + a_dst[dst], NEG_SLOPE)
            m = jax.ops.segment_max(e, dst, num_segments=n)
            e = jnp.exp(e - m[dst])
            denom = jax.ops.segment_sum(e, dst, num_segments=n)
            alpha = e / (denom[dst] + 1e-16)
            out = jax.ops.segment_sum(alpha[:, :, None] * xp[src], dst, num_segments=n)
            out = out.reshape(n, H * C) if concat else out.mean(axis=1)
            return out + bias
        h = jax.nn.elu(_gat_conv(x, edge_index, W1, att_src1, att_dst1, bias1, True))
        h = jax.nn.elu(_gat_conv(h, edge_index, W2, att_src2, att_dst2, bias2, False))
        h = (h - bn_mean) * jax.lax.rsqrt(bn_var + BN_EPS) * bn_gamma + bn_beta
        mu = h.mean(axis=-1, keepdims=True)
        var = jnp.mean((h - mu) ** 2, axis=-1, keepdims=True)
        h = (h - mu) * jax.lax.rsqrt(var + LN_EPS) * ln_gamma + ln_beta
        return h

    def _L1_ffn_ref(x, Wr, br, W1, b1, g1, be1, m1, v1, W2, b2, g2, be2, m2, v2, Wo, bo):
        import jax, jax.numpy as jnp
        import numpy as np
        BN_EPS = 0.001

        def _bn(h, g, b, m, v):
            return g * (h - m) * jax.lax.rsqrt(v + BN_EPS) + b
        feat = jnp.mean(x, axis=0)
        w = jax.nn.softmax(feat @ Wr + br, axis=-1)
        h = jnp.einsum('bfd,edh->bfeh', x, W1) + b1
        h = jax.nn.relu(_bn(h, g1, be1, m1, v1))
        h = jnp.einsum('bfeh,ehk->bfek', h, W2) + b2
        h = jax.nn.relu(_bn(h, g2, be2, m2, v2))
        y = jnp.einsum('bfeh,ehd->bfed', h, Wo) + bo
        return jnp.einsum('bfed,fe->bfd', y, w)

    def _L2_gnn_ref(h, eig, snorm_n, W1, b1, W2, b2, gamma, beta, src, dst):
        import jax, jax.numpy as jnp
        import numpy as np
        N_NODES = 50000
        N_EDGES = 25000
        D = 256
        EPS = 1e-08
        BN_EPS = 1e-05
        n = h.shape[0]
        seg = lambda x: jax.ops.segment_sum(x, dst, num_segments=n)
        z2 = jnp.concatenate([h[src], h[dst]], axis=1)
        e = z2 @ W1 + b1
        deg = seg(jnp.ones((dst.shape[0],), h.dtype))
        mean_agg = seg(e) / jnp.maximum(deg, 1.0)[:, None]
        w = eig[:, 0]
        s = seg(jnp.abs(w)) + EPS
        wn = w / s[dst]
        dir_av = seg(e * jnp.abs(wn)[:, None])
        dir_dx = jnp.abs(seg(e * wn[:, None]) - h)
        hc = jnp.concatenate([h, mean_agg, dir_av, dir_dx], axis=1)
        out = hc @ W2 + b2
        out = out * snorm_n
        mu = out.mean(axis=0)
        var = jnp.mean((out - mu) ** 2, axis=0)
        out = (out - mu) / jnp.sqrt(var + BN_EPS) * gamma + beta
        out = jax.nn.relu(out)
        out = h + out
        return out

    def _L2_ffn_ref(x, W_fx, b_fx, W_x, b_x, W_slice, b_slice, W_q, W_k, W_v, W_out, b_out, temperature):
        import jax, jax.numpy as jnp
        import numpy as np
        DIM = 256
        H = 8
        D = 64
        G = 64
        INNER = H * D
        SCALE = D ** (-0.5)
        B, N, _ = x.shape
        fx_mid = (x @ W_fx + b_fx).reshape(B, N, H, D).transpose(0, 2, 1, 3)
        x_mid = (x @ W_x + b_x).reshape(B, N, H, D).transpose(0, 2, 1, 3)
        temp = jnp.clip(temperature, 0.1, 5.0)
        slice_weights = jax.nn.softmax((x_mid @ W_slice + b_slice) / temp, axis=-1)
        slice_norm = slice_weights.sum(axis=2)
        slice_token = jnp.einsum('bhnc,bhng->bhgc', fx_mid, slice_weights)
        slice_token = slice_token / (slice_norm[..., None] + 1e-05)
        q = slice_token @ W_q
        k = slice_token @ W_k
        v = slice_token @ W_v
        attn = jax.nn.softmax(jnp.einsum('bhgc,bhkc->bhgk', q, k) * SCALE, axis=-1)
        out_slice = jnp.einsum('bhgk,bhkc->bhgc', attn, v)
        out_x = jnp.einsum('bhgc,bhng->bhnc', out_slice, slice_weights)
        out_x = out_x.transpose(0, 2, 1, 3).reshape(B, N, INNER)
        return out_x @ W_out + b_out

    def _L3_gnn_ref(x, edge_index, edge_attr, W_l, b_l, W_r, b_r, att, bias):
        import jax, jax.numpy as jnp
        import numpy as np
        N, E, D, H, C = (625, 10000, 256, 8, 32)
        NEG_SLOPE = 0.2
        n = x.shape[0]
        x_l = (x @ W_l + b_l).reshape(n, H, C)
        x_r = (x @ W_r + b_r).reshape(n, H, C)
        src, dst = (edge_index[0], edge_index[1])
        x_j = x_l[src]
        g = jax.nn.leaky_relu(x_r[dst] + x_j, NEG_SLOPE)
        alpha = jnp.einsum('ehc,hc->eh', g, att)
        alpha = alpha + jnp.log(edge_attr)[:, None]
        amax = jax.ops.segment_max(alpha, dst, num_segments=n)
        ex = jnp.exp(alpha - amax[dst])
        denom = jax.ops.segment_sum(ex, dst, num_segments=n)
        alpha = ex / (denom[dst] + 1e-16)
        out = jax.ops.segment_sum(x_j * alpha[..., None], dst, num_segments=n)
        return out.reshape(n, H * C) + bias

    def _L3_ffn_ref(features, router_w1, router_b1, router_w2, router_b2, expert_w1, expert_b1, expert_w2, expert_b2, expert_w3, expert_b3):
        import jax, jax.numpy as jnp
        import numpy as np
        E, D, H, TOP_K = (6, 256, 256, 2)
        ROUTER_H = D // 2
        rh = jax.nn.relu(features @ router_w1 + router_b1)
        expert_logits = jax.nn.softmax(rh @ router_w2 + router_b2, axis=-1)
        top_w, top_i = jax.lax.top_k(expert_logits, TOP_K)
        routing_weights = jax.nn.softmax(top_w, axis=-1)
        h1 = jax.nn.relu(jnp.einsum('bsd,edh->bseh', features, expert_w1) + expert_b1)
        h2 = jax.nn.relu(jnp.einsum('bseh,ehf->bsef', h1, expert_w2) + expert_b2)
        expert_out = jnp.einsum('bsef,efo->bseo', h2, expert_w3) + expert_b3
        sel = jnp.take_along_axis(expert_out, top_i[:, :, :, None], axis=2)
        combined = jnp.sum(sel * routing_weights[..., None], axis=2)
        return combined
    edge_index = jnp.stack([src, dst])
    x = x + _L0_gnn_ref(_layernorm(x, axis=-1), edge_attr3_1x1, L0_gnn_W, L0_gnn_w_att_src, L0_gnn_w_att_dst, src, dst)
    x = x + _L0_ffn_ref(_layernorm(x, axis=-1)[None], L0_ffn_gate_w, L0_ffn_gate_b, L0_ffn_w1, L0_ffn_b1, L0_ffn_w2, L0_ffn_b2, L0_ffn_gamma, L0_ffn_beta)[0]
    x = x + _L1_gnn_ref(_layernorm(x, axis=-1), edge_index, L1_gnn_W1, L1_gnn_att_src1, L1_gnn_att_dst1, L1_gnn_bias1, L1_gnn_W2, L1_gnn_att_src2, L1_gnn_att_dst2, L1_gnn_bias2, L1_gnn_bn_gamma, L1_gnn_bn_beta, L1_gnn_bn_mean, L1_gnn_bn_var, L1_gnn_ln_gamma, L1_gnn_ln_beta)
    x = x + _L1_ffn_ref(_layernorm(x, axis=-1)[None], L1_ffn_Wr, L1_ffn_br, L1_ffn_W1, L1_ffn_b1, L1_ffn_g1, L1_ffn_be1, L1_ffn_m1, L1_ffn_v1, L1_ffn_W2, L1_ffn_b2, L1_ffn_g2, L1_ffn_be2, L1_ffn_m2, L1_ffn_v2, L1_ffn_Wo, L1_ffn_bo)[0]
    x = x + _L2_gnn_ref(_layernorm(x, axis=-1), edge_attr_2, node_vec1, L2_gnn_W1, L2_gnn_b1, L2_gnn_W2, L2_gnn_b2, L2_gnn_gamma, L2_gnn_beta, src, dst)
    x = x + _L2_ffn_ref(_layernorm(x, axis=-1)[None], L2_ffn_W_fx, L2_ffn_b_fx, L2_ffn_W_x, L2_ffn_b_x, L2_ffn_W_slice, L2_ffn_b_slice, L2_ffn_W_q, L2_ffn_W_k, L2_ffn_W_v, L2_ffn_W_out, L2_ffn_b_out, L2_ffn_temperature)[0]
    x = x + _L3_gnn_ref(_layernorm(x, axis=-1), edge_index, edge_weight, L3_gnn_W_l, L3_gnn_b_l, L3_gnn_W_r, L3_gnn_b_r, L3_gnn_att, L3_gnn_bias)
    x = x + _L3_ffn_ref(_layernorm(x, axis=-1)[None], L3_ffn_router_w1, L3_ffn_router_b1, L3_ffn_router_w2, L3_ffn_router_b2, L3_ffn_expert_w1, L3_ffn_expert_b1, L3_ffn_expert_w2, L3_ffn_expert_b2, L3_ffn_expert_w3, L3_ffn_expert_b3)[0]
    return x

_drawn_inputs = setup_inputs


def setup_inputs(seed=0):
    import zlib

    import numpy as np

    out = dict(_drawn_inputs(seed))
    spreads = {'L0_ffn_gate_b': (0.0, 0.1),
     'L0_ffn_b1': (0.0, 0.678),
     'L0_ffn_b2': (0.0, 0.1),
     'L0_ffn_gamma': (1.0, 0.2),
     'L0_ffn_beta': (0.0, 0.1),
     'L1_gnn_bias1': (0.0, 0.1),
     'L1_gnn_bias2': (0.0, 0.1),
     'L1_gnn_bn_gamma': (1.0, 0.2),
     'L1_gnn_bn_beta': (0.0, 0.1),
     'L1_gnn_bn_var': (1.0, 0.2),
     'L1_gnn_ln_gamma': (1.0, 0.2),
     'L1_gnn_ln_beta': (0.0, 0.1),
     'L1_ffn_br': (0.0, 0.8),
     'L1_ffn_b1': (0.0, 0.634),
     'L1_ffn_g1': (1.0, 0.6),
     'L1_ffn_be1': (0.0, 0.702),
     'L1_ffn_m1': (0.0, 0.651),
     'L1_ffn_v1': (1.0, 0.6),
     'L1_ffn_b2': (0.0, 0.48),
     'L1_ffn_g2': (1.0, 0.6),
     'L1_ffn_be2': (0.0, 0.53),
     'L1_ffn_m2': (0.0, 0.477),
     'L1_ffn_v2': (1.0, 0.6),
     'L1_ffn_bo': (0.0, 0.36),
     'L2_gnn_b1': (0.0, 0.735),
     'L2_gnn_b2': (0.0, 0.675),
     'L2_gnn_gamma': (1.0, 0.2),
     'L2_gnn_beta': (0.0, 0.356),
     'L2_ffn_b_fx': (0.0, 0.267),
     'L2_ffn_b_x': (0.0, 0.8),
     'L2_ffn_b_slice': (0.0, 0.8),
     'L2_ffn_b_out': (0.0, 0.1),
     'L2_ffn_temperature': (0.5, 0.6),
     'L3_ffn_router_b1': (0.0, 0.675),
     'L3_ffn_router_b2': (0.0, 0.56),
     'L3_ffn_expert_b1': (0.0, 0.8),
     'L3_ffn_expert_b2': (0.0, 0.8),
     'L3_ffn_expert_b3': (0.0, 0.405)}
    factors = {'L1_gnn_att_dst1': 5.555,
     'L1_gnn_att_src2': 2.893,
     'L1_gnn_att_dst2': 8.0,
     'L2_ffn_W_x': 8.0,
     'L2_ffn_W_slice': 8.0,
     'L2_ffn_W_q': 8.0,
     'L2_ffn_W_k': 8.0,
     'L3_gnn_b_l': 8.0,
     'L3_gnn_b_r': 54.114,
     'L3_gnn_bias': 8.0,
     'L3_ffn_expert_w1': 3.854,
     'L3_ffn_expert_w2': 3.318}
    for name, (base, spread) in spreads.items():
        noise = np.random.default_rng([zlib.crc32(name.encode()), seed]).standard_normal(out[name].shape)
        drawn = base * np.exp(spread * noise) if base else spread * noise
        out[name] = jnp.asarray(drawn.astype(out[name].dtype))
    for name, factor in factors.items():
        out[name] = (out[name] * factor).astype(out[name].dtype)
    return out
```

```python
from contextlib import ExitStack

import numpy as np

import concourse.bass as bass
from concourse import mybir

F32 = mybir.dt.float32
BF16 = mybir.dt.bfloat16
I32 = mybir.dt.int32
I16 = mybir.dt.int16
ALU = mybir.AluOpType
ACT = mybir.ActivationFunctionType
AX = mybir.AxisListType.X

P = 128
NODES = 3125
D = 256
KD = D // P
TILES = -(-NODES // P)
ROWS = TILES * P
LAST = NODES - (TILES - 1) * P
EDGES = 50000
SUB = 4
CHUNK = SUB * P
CHUNKS = -(-EDGES // CHUNK)
FULL = EDGES // CHUNK
TAIL = EDGES - FULL * CHUNK
RING = 4
SLOTS = -(-(CHUNKS + 1) // RING) * RING
PAIRS_MAX = 2560
NEVER = -1.0e30
SLOPE = 0.2
BANKS = 5


class Phase(ExitStack):

    def __init__(self, nc):
        super().__init__()
        self.nc, self.semaphores = nc, []

    def semaphore(self, name):
        self.semaphores.append(self.nc.alloc_semaphore(name))
        return self.semaphores[-1]

    def __exit__(self, *error):
        super().__exit__(*error)
        if self.semaphores:
            self.nc.clear_and_free_semaphores(self.semaphores)
            self.nc.all_engine_barrier()
        return False


def persistent(nc, ctx):
    def sb(name, shape, dt):
        return ctx.enter_context(nc.sbuf_tensor(name, shape, dt))

    class Buffers:
        pass

    b = Buffers()
    b.x = sb("x_stream", [P, TILES, D], F32)
    b.xnT = sb("xnT", [P, KD, ROWS], F32)
    b.ident = sb("ident", [P, P], F32)
    b.node_iota = sb("node_iota", [P, ROWS], F32)
    b.node_id = sb("node_id", [P, TILES], F32)
    b.head_rows = sb("head_rows", [40, 8, P], BF16)
    b.src_id = sb("src_id", [P, SLOTS, SUB], I32)
    b.dst_id = sb("dst_id", [P, SLOTS, SUB], F32)
    b.edge_dist = sb("edge_dist", [P, SLOTS, SUB], F32)
    b.edge_dir = sb("edge_dir", [P, SLOTS, SUB], F32)
    b.edge_logw = sb("edge_logw", [P, SLOTS, SUB], F32)
    b.pair_list = sb("pair_list", [1, PAIRS_MAX], I32)
    b.gate_list = sb("gate_list", [1, SLOTS], I32)
    b.half_pairs = sb("half_pairs", [1, 2], I32)
    b.ones = sb("ones", [P, 1], F32)
    b.dst_dram = nc.dram_tensor("dst_padded", (SLOTS, CHUNK), I16, kind="Internal").ap()
    widths = [("att0", 260), ("att1", 260), ("att2", 257), ("dir", 257), ("att3", 264)]
    b.table = {n: nc.dram_tensor(f"table_{n}", (ROWS, w), F32, kind="Internal").ap() for n, w in widths}
    return b


def prepare(nc, b, x, src, dst, dist, attr2, weight):
    with Phase(nc) as ctx:
        def sb(name, shape, dt):
            return ctx.enter_context(nc.sbuf_tensor(name, shape, dt))

        def sem(name):
            return ctx.semaphore(name)

        src_rows = sb("src_rows", [SLOTS, CHUNK], I32)
        dst_rows = sb("dst_rows", [SLOTS, CHUNK], I32)
        dst_high = sb("dst_high", [SLOTS, CHUNK], I32)
        dist_rows = sb("dist_rows", [SLOTS, CHUNK], F32)
        dir_rows = sb("dir_rows", [SLOTS, 2 * CHUNK], F32)
        weight_rows = sb("weight_rows", [SLOTS, CHUNK], F32)
        logw_rows = sb("logw_rows", [SLOTS, CHUNK], F32)
        src_f = sb("src_f", [SLOTS, CHUNK], F32)
        dst_f = sb("dst_f", [SLOTS, CHUNK], F32)
        dst_h = sb("dst_h", [SLOTS, CHUNK], I16)
        span_i = sb("span_i", [SLOTS, 2], I32)
        span_w = sb("span_w", [SLOTS, 2], I32)
        span_f = sb("span_f", [SLOTS, 2], F32)
        head_iota = sb("head_iota", [40, 8, P], F32)
        head_id = sb("head_id", [40, 2], F32)
        row = sb("row", [1, 8, P], F32)
        zero_row = sb("zero_row", [1, P], F32)
        step_col = sb("step_col", [SLOTS, 2], F32)
        pair_iota = sb("pair_iota", [SLOTS, PAIRS_MAX], F32)
        mask = sb("mask", [SLOTS, PAIRS_MAX], F32)
        pair_f = sb("pair_f", [1, 4, PAIRS_MAX], F32)
        half_bits = sb("half_bits", [1, 2], I32)
        ps_turn = ctx.enter_context(nc.psum_tensor("ps_turn", [P, SUB, P], F32))
        ps_row = ctx.enter_context(nc.psum_tensor("ps_row", [P, 4, P], F32))
        ps_col = ctx.enter_context(nc.psum_tensor("ps_col", [P, P], F32))
        ps_pair = ctx.enter_context(nc.psum_tensor("ps_pair", [1, 512], F32))
        ps_pair2 = ctx.enter_context(nc.psum_tensor("ps_pair2", [1, 512], F32))

        filled = sem("filled")
        loaded = sem("loaded")
        x_loaded = sem("x_loaded")
        iota_done = sem("iota_done")
        const_done = sem("const_done")
        turned = sem("turned")
        turn_kept = sem("turn_kept")
        logged = sem("logged")
        rows_cast = sem("rows_cast")
        dst_kept = sem("dst_kept")
        spans_ready = sem("spans_ready")
        spans_turned = sem("spans_turned")
        cols_ready = sem("cols_ready")
        cols_turned = sem("cols_turned")
        mask_ready = sem("mask_ready")
        pairs_summed = sem("pairs_summed")
        pairs_kept = sem("pairs_kept")

        def flat(a):
            return a.rearrange("(c e) -> c e", e=CHUNK)

        block = ctx.enter_context(nc.Block())

        @block.sync
        def _(sp):
            sp.wait_ge(filled, 1)
            sp.dma_start(b.x[:, 0:TILES - 1, :],
                         x[0:(TILES - 1) * P, :].rearrange("(t p) d -> p t d", p=P)).then_inc(x_loaded, 16)
            sp.dma_start(b.x[0:LAST, TILES - 1, :], x[(TILES - 1) * P:NODES, :]).then_inc(x_loaded, 16)
            sp.wait_ge(filled, 7)
            edge_loads = [(dst_rows, dst, 1), (dst_high, dst, 1), (src_rows, src, 1),
                          (dist_rows, dist, 1), (dir_rows, attr2, 2), (weight_rows, weight, 1)]
            for rows, a, width in edge_loads:
                full, tail = FULL * CHUNK * width, TAIL * width
                sp.dma_start(rows[0:FULL, :],
                             a[0:full].rearrange("(c e) -> c e", e=CHUNK * width)).then_inc(loaded, 16)
                sp.dma_start(rows[FULL:FULL + 1, 0:tail],
                             a[full:full + tail].rearrange("(c e) -> c e", c=1)).then_inc(loaded, 16)
            sp.wait_ge(rows_cast, 1)
            sp.dma_start(b.dst_dram, dst_h[:]).then_inc(dst_kept, 16)
            sp.wait_ge(dst_kept, 16)
            sp.wait_ge(x_loaded, 32)

        @block.gpsimd
        def _(pool):
            pool.memset(b.x[:, TILES - 1, :], 0.0).then_inc(filled, 1)
            pool.memset(dst_rows[:], -1).then_inc(filled, 1)
            pool.memset(dst_high[:], 1 << 14).then_inc(filled, 1)
            pool.memset(src_rows[:], 0).then_inc(filled, 1)
            pool.memset(dist_rows[:], 0.0).then_inc(filled, 1)
            pool.memset(dir_rows[:], 0.0).then_inc(filled, 1)
            pool.memset(weight_rows[:], 1.0).then_inc(filled, 1)
            pool.memset(b.ones[:], 1.0).then_inc(iota_done, 1)
            pool.memset(zero_row[:], 0.0).then_inc(iota_done, 1)
            pool.iota(b.node_iota[:], [[1, ROWS]], base=0, channel_multiplier=0,
                      allow_small_or_imprecise_dtypes=True).then_inc(iota_done, 1)
            pool.iota(b.node_id[:], [[P, TILES]], base=0, channel_multiplier=1,
                      allow_small_or_imprecise_dtypes=True).then_inc(iota_done, 1)
            pool.iota(head_iota[:], [[1, 8], [0, P]], base=0, channel_multiplier=0,
                      allow_small_or_imprecise_dtypes=True).then_inc(iota_done, 1)
            pool.iota(head_id[:, 0:1], [[1, 1]], base=0, channel_multiplier=1,
                      allow_small_or_imprecise_dtypes=True).then_inc(iota_done, 1)
            pool.iota(head_id[:, 1:2], [[1, 1]], base=-32, channel_multiplier=1,
                      allow_small_or_imprecise_dtypes=True).then_inc(iota_done, 1)
            pool.iota(pair_iota[:], [[1, PAIRS_MAX]], base=0, channel_multiplier=0,
                      allow_small_or_imprecise_dtypes=True).then_inc(iota_done, 1)

        @block.scalar
        def _(act):
            act.wait_ge(loaded, 12 * 16)
            act.activation(logw_rows[:], weight_rows[:], ACT.Ln).then_inc(logged, 1)

        @block.vector
        def _(dve):
            dve.wait_ge(iota_done, 8)
            dve.tensor_scalar(b.ident[:], b.node_iota[:, 0:P], b.node_id[:, 0:1], None,
                              ALU.is_equal).then_inc(const_done, 1)
            dve.tensor_scalar(head_iota[:, :, 64:P], head_iota[:, :, 0:64], head_id[:, 0:1], None,
                              ALU.is_equal)
            dve.drain()
            dve.scalar_tensor_tensor(b.head_rows[:, :, 0:64], head_iota[:, :, 0:64], head_id[:, 1:2],
                                     head_iota[:, :, 64:P], ALU.is_equal, ALU.add)
            dve.scalar_tensor_tensor(b.head_rows[:, :, 64:P], head_iota[:, :, 0:64], head_id[:, 1:2],
                                     head_iota[:, :, 64:P], ALU.is_equal, ALU.add)
            dve.wait_ge(loaded, 12 * 16)
            dve.tensor_copy(dst_f[:], dst_rows[:])
            dve.tensor_copy(src_f[:], src_rows[:])
            dve.tensor_copy(dst_h[:], dst_rows[:]).then_inc(rows_cast, 1)
            dve.tensor_reduce(span_i[:, 0:1], dst_high[:], AX, ALU.min)
            dve.tensor_reduce(span_i[:, 1:2], dst_rows[:], AX, ALU.max)
            dve.drain()
            dve.tensor_scalar(span_w[:], span_i[:], 7, None, ALU.arith_shift_right)
            dve.drain()
            dve.tensor_copy(span_f[:], span_w[:])
            dve.drain()
            dve.tensor_scalar(span_f[:], span_f[:], float(TILES - 1), None, ALU.min).then_inc(spans_ready, 1)
            tables = [b.dst_id, b.src_id, b.edge_dist, b.edge_dir, b.edge_logw]
            for n, table in enumerate(tables):
                dve.wait_ge(turned, n + 1)
                dve.tensor_copy(table[:].rearrange("p c j -> p j c"),
                                ps_turn[:, :, 0:SLOTS]).then_inc(turn_kept, 1)
            dve.wait_ge(spans_turned, 1)
            first, last, count, upto, before, shift, step = (row[:, i, 0:SLOTS] for i in range(7))
            dve.tensor_copy(row[:, 0:2, 0:SLOTS], ps_row[0:1, 0:2, 0:SLOTS])
            dve.memset(row[:, 2:8, :], 0.0)
            dve.drain()
            dve.scalar_tensor_tensor(row[:, 2, 0:CHUNKS], row[:, 1, 0:CHUNKS], 1.0, row[:, 0, 0:CHUNKS],
                                     ALU.add, ALU.subtract)
            dve.drain()
            dve.tensor_tensor_scan(upto, count, zero_row[:, 0:SLOTS], 0.0, ALU.add, ALU.add)
            dve.drain()
            dve.tensor_tensor(before, upto, count, ALU.subtract)
            dve.drain()
            dve.tensor_tensor(shift, before, first, ALU.subtract)
            dve.tensor_scalar(b.gate_list[:, RING:SLOTS], row[:, 4, 1:SLOTS - RING + 1], 1.0, None, ALU.add)
            dve.memset(b.gate_list[:, 0:RING], 1)
            dve.tensor_copy(half_bits[:, 0:1], row[:, 3, SLOTS - 1:SLOTS])
            dve.drain()
            dve.tensor_scalar(b.half_pairs[:, 0:1], half_bits[:, 0:1], 1, None, ALU.arith_shift_right)
            dve.tensor_tensor(row[:, 6, 0:CHUNKS - 1], row[:, 5, 1:CHUNKS], row[:, 5, 0:CHUNKS - 1],
                              ALU.subtract).then_inc(cols_ready, 1)
            dve.wait_ge(cols_turned, 1)
            dve.tensor_copy(step_col[:], ps_col[0:SLOTS, 0:2])
            dve.drain()
            dve.tensor_scalar(mask[0:CHUNKS, :], pair_iota[0:CHUNKS, :], step_col[0:CHUNKS, 0:1], None,
                              ALU.is_ge).then_inc(mask_ready, 1)
            for n in range(PAIRS_MAX // 512):
                cols = slice(512 * n, 512 * n + 512)
                dve.wait_ge(pairs_summed, n + 1)
                dve.tensor_scalar(pair_f[:, 0, cols], ps_pair[:], 32.0, None, ALU.mult)
                dve.scalar_tensor_tensor(pair_f[:, 1, cols], ps_pair2[:], row[:, 5, 0:1],
                                         pair_iota[0:1, cols], ALU.add, ALU.subtract).then_inc(pairs_kept, 1)
            dve.drain()
            dve.tensor_scalar(pair_f[:, 2, :], pair_f[:, 1, :], -1.0, float(TILES - 1), ALU.mult, ALU.min)
            dve.drain()
            dve.tensor_tensor(b.pair_list[:], pair_f[:, 2, :], pair_f[:, 0, :], ALU.add)

        @block.tensor
        def _(pe):
            pe.wait_ge(const_done, 1)
            pe.wait_ge(rows_cast, 1)
            rows = [dst_f, src_f, dist_rows, None, logw_rows]
            for n in range(5):
                if n:
                    pe.wait_ge(turn_kept, n)
                if n == 4:
                    pe.wait_ge(logged, 1)
                for j in range(SUB):
                    if n == 3:
                        a = dir_rows[:, 2 * P * j:2 * P * (j + 1):2]
                    else:
                        a = rows[n][:, P * j:P * (j + 1)]
                    mm = pe.transpose(ps_turn[:, j, 0:SLOTS], a, b.ident[0:SLOTS, 0:SLOTS])
                mm.then_inc(turned, 1)
            pe.wait_ge(spans_ready, 1)
            pe.transpose(ps_row[0:1, 0, 0:SLOTS], span_f[:, 0:1], b.ident[0:SLOTS, 0:SLOTS])
            pe.transpose(ps_row[0:1, 1, 0:SLOTS], span_f[:, 1:2], b.ident[0:SLOTS, 0:SLOTS]).then_inc(spans_turned, 1)
            pe.wait_ge(cols_ready, 1)
            pe.transpose(ps_col[0:SLOTS, 0:1], row[:, 3, 0:SLOTS], b.ident[0:1, 0:1])
            pe.transpose(ps_col[0:SLOTS, 1:2], row[:, 6, 0:SLOTS], b.ident[0:1, 0:1]).then_inc(cols_turned, 1)
            pe.wait_ge(mask_ready, 1)
            for n in range(PAIRS_MAX // 512):
                cols = slice(512 * n, 512 * n + 512)
                if n:
                    pe.wait_ge(pairs_kept, n)
                pe.matmul(ps_pair[:], b.ones[0:CHUNKS, :], mask[0:CHUNKS, cols], start=True, stop=True)
                pe.matmul(ps_pair2[:], step_col[0:CHUNKS, 1:2], mask[0:CHUNKS, cols],
                          start=True, stop=True).then_inc(pairs_summed, 1)


def normalize(nc, b, name, keep=None):
    with Phase(nc) as ctx:
        stats = ctx.enter_context(nc.sbuf_tensor(f"{name}_stats", [P, TILES, 6], F32))
        moments = ctx.enter_context(nc.sbuf_tensor(f"{name}_moments", [P, TILES, 2], F32))
        spread = ctx.enter_context(nc.sbuf_tensor(f"{name}_spread", [P, TILES], F32))
        scale = ctx.enter_context(nc.sbuf_tensor(f"{name}_scale", [P, TILES], F32))
        if keep is None:
            keep = ctx.enter_context(nc.sbuf_tensor(f"{name}_xn", [P, TILES, D], F32))
        ps_t = ctx.enter_context(nc.psum_tensor(f"{name}_ps_t", [P, BANKS, 2, KD, P], F32))
        moments_ready = ctx.semaphore(f"{name}_moments_ready")
        spread_ready = ctx.semaphore(f"{name}_spread_ready")
        tile_ready = ctx.semaphore(f"{name}_tile_ready")
        tile_turned = ctx.semaphore(f"{name}_tile_turned")
        bank_free = ctx.semaphore(f"{name}_bank_free")
        block = ctx.enter_context(nc.Block())

        @block.vector
        def _(dve):
            if keep.shape[2] > D:
                dve.memset(keep[:, :, D:], 1.0)
            with dve.Fori(0, TILES) as t:
                dve.bn_stats(stats[:, bass.ds(t, 1), :].rearrange("p t s -> p (t s)"),
                             b.x[:, bass.ds(t, 1), :].rearrange("p t d -> p (t d)"))
            dve.drain()
            for t in range(TILES):
                dve.bn_aggr(moments[:, t, :], stats[:, t, :])
            dve.drain()
            dve.tensor_scalar(spread[:], moments[:, :, 1], 1e-5, None, ALU.add).then_inc(moments_ready, 1)
            dve.wait_ge(spread_ready, 1)
            dve.reciprocal(scale[:], scale[:])
            dve.drain()
            with dve.Fori(0, TILES) as t:
                dve.tensor_scalar(keep[:, bass.ds(t, 1), 0:D].rearrange("p t d -> p (t d)"),
                                  b.x[:, bass.ds(t, 1), :].rearrange("p t d -> p (t d)"),
                                  moments[:, bass.ds(t, 1), 0], scale[:, bass.ds(t, 1)],
                                  ALU.subtract, ALU.mult).then_inc(tile_ready, 1)

        @block.scalar
        def _(act):
            act.sem_inc(bank_free, BANKS)
            act.wait_ge(moments_ready, 1)
            act.activation(scale[:], spread[:], ACT.Sqrt).then_inc(spread_ready, 1)
            with act.Fori(0, TILES // BANKS) as i:
                for u in range(BANKS):
                    t = i * BANKS + u
                    act.wait_ge(tile_turned, t + 1)
                    act.activation(b.xnT[:, :, bass.ds(t * P, P)], ps_t[:, u, 0, :, :],
                                   ACT.Identity).then_inc(bank_free, 1)

        @block.tensor
        def _(pe):
            for t in range(TILES):
                pe.wait_ge(tile_ready, t + 1)
                pe.wait_ge(bank_free, t + 1)
                for k in range(KD):
                    mm = pe.transpose(ps_t[:, t % BANKS, 0, k, :], keep[:, t, k * P:(k + 1) * P], b.ident[:])
                mm.then_inc(tile_turned, 1)


def per_window(a):
    return a.rearrange("p t d -> p (t d)")


def attention_tables(nc, b, name, weights, att_src, att_dst, heads, table, acc, best, dst_part, loops):
    width = D // heads
    cols = D + 2 * heads
    with Phase(nc) as ctx:
        def sb(nm, shape, dt=F32):
            return ctx.enter_context(nc.sbuf_tensor(f"{name}_{nm}", shape, dt))

        def sem(nm):
            return ctx.semaphore(f"{name}_{nm}")

        w = sb("w", [P, KD, cols])
        att = sb("att", [P, 2, D])
        prod = sb("prod", [P, KD, 2, D])
        stage = sb("stage", [P, BANKS, D + heads])
        ps = ctx.enter_context(nc.psum_tensor(f"{name}_ps", [P, BANKS, 512], F32))
        loaded = sem("loaded")
        folded = sem("folded")
        projected = sem("projected")
        staged = sem("staged")
        kept = sem("kept")
        stored = [sem(f"stored{u}") for u in range(BANKS)]
        block = ctx.enter_context(nc.Block())

        @block.sync
        def _(sp):
            sp.dma_start(w[:, :, 0:D], weights.rearrange("(k p) n -> p k n", p=P)).then_inc(loaded, 16)
            sp.dma_start(att[:, 0, :], att_src.partition_broadcast(P)).then_inc(loaded, 16)
            sp.dma_start(att[:, 1, :], att_dst.partition_broadcast(P)).then_inc(loaded, 16)
            for u in range(BANKS):
                sp.sem_inc(stored[u], 16)
            with sp.Fori(0, TILES // BANKS) as i:
                for u in range(BANKS):
                    t = i * BANKS + u
                    sp.wait_ge(staged, t + 1)
                    sp.dma_start(table[bass.ds(t * P, P), :], stage[:, u, :]).then_inc(stored[u], 16)
            for u in range(BANKS):
                sp.wait_ge(stored[u], 16 * (TILES // BANKS + 1))

        @block.tensor
        def _(pe):
            pe.wait_ge(folded, 1)
            for t in range(TILES):
                pe.wait_ge(kept, t + 1)
                for k in range(KD):
                    mm = pe.matmul(ps[:, t % BANKS, 0:cols], b.xnT[:, k, t * P:(t + 1) * P], w[:, k, :],
                                   start=(k == 0), stop=(k == KD - 1))
                mm.then_inc(projected, 1)

        @block.scalar
        def _(act):
            with act.Fori(0, TILES // BANKS) as i:
                for u in range(BANKS):
                    t = i * BANKS + u
                    act.wait_ge(projected, t + 1)
                    act.wait_ge(stored[u], (i + 1) * 16)
                    act.activation(stage[:, u, :], ps[:, u, 0:D + heads], ACT.Identity).then_inc(staged, 1)

        @block.vector
        def _(dve):
            dve.sem_inc(kept, BANKS)
            if loops:
                dve.memset(acc[:, :, :, width], 1.0)
            else:
                dve.memset(acc[:], 0.0)
                dve.memset(best[:], NEVER)
            dve.wait_ge(loaded, 48)
            for k in range(KD):
                for s in range(2):
                    dve.tensor_tensor(prod[:, k, s, :], w[:, k, 0:D], att[:, s, :], ALU.mult)
            dve.drain()
            for k in range(KD):
                ins = dve.tensor_reduce(w[:, k, D:cols], prod[:, k, :, :].rearrange(
                    "p s (h c) -> p (s h) c", c=width), AX, ALU.add)
            ins.then_inc(folded, 1)
            with dve.Fori(0, TILES // BANKS) as i:
                for u in range(BANKS):
                    t = i * BANKS + u
                    dve.wait_ge(staged, t + 1)
                    own = dst_part[:, bass.ds(t, 1), :].rearrange("p t h -> p (t h)")
                    if not loops:
                        dve.tensor_copy(own, ps[:, u, D + heads:cols]).then_inc(kept, 1)
                        continue
                    top = best[:, bass.ds(t, 1), :].rearrange("p t h -> p (t h)")
                    mine = acc[:, bass.ds(t, 1), :, :].rearrange("p t h c -> p (t h) c")
                    dve.tensor_copy(own, ps[:, u, D + heads:cols])
                    dve.tensor_copy(mine[:, :, 0:width],
                                    ps[:, u, 0:D].rearrange("p (h c) -> p h c", c=width))
                    dve.drain()
                    dve.tensor_tensor(top, ps[:, u, D:D + heads], own, ALU.add)
                    dve.drain()
                    dve.scalar_tensor_tensor(top, top, SLOPE, top, ALU.mult, ALU.max).then_inc(kept, 1)


def pair_at(eng, b, k):
    v = eng.value_load(b.pair_list[0:1, bass.ds(k, 1)], min_val=0, max_val=CHUNKS * 32 + 31)
    c = eng.snap(v >> 5)
    w = eng.snap((v & 31).with_bounds(min_val=0, max_val=TILES - 1))
    return c, w


def load_chunks(nc, b, ctx, name, width, b_done):
    g = ctx.enter_context(nc.sbuf_tensor(f"{name}_g", [P, RING, SUB, width], F32))
    dst_b = ctx.enter_context(nc.sbuf_tensor(f"{name}_dst_b", [P, RING, CHUNK], I16))
    ids = ctx.enter_context(nc.sbuf_tensor(f"{name}_ids", [P, RING, SUB], I32))
    gathered = [ctx.semaphore(f"{name}_gathered{u}") for u in range(RING)]
    landed = [ctx.semaphore(f"{name}_landed{u}") for u in range(RING)]
    ids_ready = ctx.semaphore(f"{name}_ids_ready")
    ids_seen = ctx.semaphore(f"{name}_ids_seen")
    g_ready = ctx.semaphore(f"{name}_g_ready")
    dst_ready = ctx.semaphore(f"{name}_dst_ready")

    def pool_program(pool, table):
        def fetch(i, u, start=False):
            c = i * RING + u
            if not start:
                gate = pool.value_load(b.gate_list[0:1, bass.ds(c, 1)], min_val=1, max_val=PAIRS_MAX)
                pool.wait_ge(b_done, gate)
            pool.tensor_copy(ids[:, u, :], b.src_id[:, bass.ds(c, 1), :].rearrange(
                "p c j -> p (c j)")).then_inc(ids_ready, 1)
            pool.wait_ge(ids_ready, c + 1)
            pool.sem_inc(ids_seen, 1)
            for j in range(SUB):
                pool.indirect_dma_start(
                    out=g[:, u, j, :], out_offset=None, in_=table,
                    in_offset=bass.IndirectOffsetOnAxis(ap=ids[:, u, j:j + 1], axis=0)).then_inc(gathered[u], 16)
            if u:
                pool.wait_ge(gathered[u - 1], (i + 1) * (16 * SUB))
                pool.sem_inc(g_ready, 1)
            elif not start:
                pool.wait_ge(gathered[RING - 1], i * (16 * SUB))
                pool.sem_inc(g_ready, 1)

        for u in range(RING):
            fetch(0, u, True)
        with pool.Fori(1, SLOTS // RING) as i:
            for u in range(RING):
                fetch(i, u)
        pool.wait_ge(gathered[RING - 1], SLOTS // RING * 16 * SUB)
        pool.sem_inc(g_ready, 1)

    def sp_program(sp):
        def fetch(i, u, start=False):
            c = i * RING + u
            if not start:
                gate = sp.value_load(b.gate_list[0:1, bass.ds(c, 1)], min_val=1, max_val=PAIRS_MAX)
                sp.wait_ge(b_done, gate)
            sp.dma_start(dst_b[:, u, :], b.dst_dram[bass.ds(c, 1), :].rearrange(
                "c e -> (c e)").partition_broadcast(P)).then_inc(landed[u], 16)
            if u:
                sp.wait_ge(landed[u - 1], (i + 1) * 16)
                sp.sem_inc(dst_ready, 1)
            elif not start:
                sp.wait_ge(landed[RING - 1], i * 16)
                sp.sem_inc(dst_ready, 1)

        for u in range(RING):
            fetch(0, u, True)
        with sp.Fori(1, SLOTS // RING) as i:
            for u in range(RING):
                fetch(i, u)
        sp.wait_ge(landed[RING - 1], SLOTS // RING * 16)
        sp.sem_inc(dst_ready, 1)

    return g, dst_b, g_ready, dst_ready, pool_program, sp_program


def attend(nc, b, name, heads, table, acc, best, dst_part, use_dist=False, pair_dots=None):
    width = D // heads
    group = width + 1
    row_width = D + heads
    with Phase(nc) as ctx:
        def sb(nm, shape, dt=F32):
            return ctx.enter_context(nc.sbuf_tensor(f"{name}_{nm}", shape, dt))

        def pb(nm, shape):
            return ctx.enter_context(nc.psum_tensor(f"{name}_{nm}", shape, F32))

        def sem(nm):
            return ctx.semaphore(f"{name}_{nm}")

        b_done = sem("b_done")
        g, dst_b, g_ready, dst_ready, pool_program, sp_program = load_chunks(
            nc, b, ctx, name, row_width, b_done)

        st = sb("st", [P, 2, CHUNK])
        out_of = sb("out_of", [P, 2, CHUNK])
        s = sb("s", [P, 2, SUB, P])
        score_rows = sb("score_rows", [40, 2, CHUNK], BF16)
        masked = sb("masked", [P, 2, CHUNK], BF16)
        top = sb("top", [P, 2, heads])
        cand = sb("cand", [P, 2, heads])
        node_side = sb("node_side", [P, 2, 2 * heads])
        drop = sb("drop", [P, 2, heads])
        shrink = sb("shrink", [P, 2, heads])
        shrink_kept = sb("shrink_kept", [P, 2, heads])
        arg = sb("arg", [P, 2, SUB, heads])
        arg2 = sb("arg2", [P, 2, SUB, heads])
        ex = sb("ex", [P, 2, SUB, heads])
        exd = sb("exd", [P, 2, SUB, heads])
        rows = sb("rows", [P, 2, SUB, heads, group])
        alpha = sb("alpha", [P, 2, SUB, heads])
        if pair_dots:
            x_r, att = pair_dots
            mixed = sb("mixed", [P, 2, SUB, D])
            bent = sb("bent", [P, 2, SUB, heads])
            ps_x = pb("ps_x", [P, SUB, D])
        ps_t = pb("ps_t", [heads, CHUNK])
        ps_v = pb("ps_v", [P, 2, CHUNK])
        ps_m = pb("ps_m", [P, SUB, P])
        ps_o = pb("ps_o", [P, 2, 512])

        st_ready = sem("st_ready")
        mix_summed = sem("mix_summed")
        alpha_ready = sem("alpha_ready")
        scores_turned = sem("scores_turned")
        high_ready = sem("high_ready")
        low_ready = sem("low_ready")
        spread_ready = sem("spread_ready")
        spread_free = sem("spread_free")
        held = sem("held")
        node_ready = sem("node_ready")
        shrink_ready = sem("shrink_ready")
        edge_ready = sem("edge_ready")
        arg_ready = sem("arg_ready")
        ex_ready = sem("ex_ready")
        summed = sem("summed")
        cleared = sem("cleared")

        def run_pairs(eng, first, step):
            half = eng.value_load(b.half_pairs[0:1, 0:1], min_val=1, max_val=PAIRS_MAX // 2 - 2)
            first()
            with eng.Fori(0, half) as i:
                for u in (1, 2):
                    step(i * 2 + u, u % 2)
            return half

        block = ctx.enter_context(nc.Block())

        @block.gpsimd
        def _(pool):
            pool_program(pool, table)

        @block.sync
        def _(sp):
            sp_program(sp)

        @block.tensor
        def _(pe):
            def mix(k, p, c, w):
                pe.wait_ge(st_ready, k + 1)
                for j in range(SUB):
                    mm = pe.matmul(ps_x[:, j, :], st[:, p, j * P:(j + 1) * P],
                                   x_r[:, bass.ds(w, 1), :].rearrange("p t d -> p (t d)"),
                                   start=True, stop=True)
                mm.then_inc(mix_summed, 1)

            def turn(k, p, c, w):
                pe.wait_ge(alpha_ready, k + 1)
                for j in range(SUB):
                    mm = pe.transpose(ps_t[:, j * P:(j + 1) * P], alpha[:, p, j, :], b.ident[:])
                mm.then_inc(scores_turned, 1)

            def spread(k, p):
                pe.wait_ge(low_ready, k + 1)
                for h in range(heads):
                    pe.wait_ge(spread_free, k * heads + h + 1)
                    pe.matmul(ps_v[:, (p * heads + h) % 2, :], b.head_rows[:, h, :], score_rows[:, p, :],
                              start=True, stop=True).then_inc(spread_ready, 1)

            def to_edges(k, p):
                pe.wait_ge(node_ready, k + 1)
                for j in range(SUB):
                    mm = pe.matmul(ps_m[:, j, 0:2 * heads], st[:, p, j * P:(j + 1) * P],
                                   node_side[:, p, :], start=True, stop=True)
                mm.then_inc(edge_ready, 1)

            def scatter(k, p):
                pe.wait_ge(b_done, k + 2)
                for j in range(SUB):
                    mm = pe.matmul(ps_o[:, p, 0:heads * group], s[:, p, j, :],
                                   rows[:, p, j, :, :].rearrange("p h c -> p (h c)"),
                                   start=(j == 0), stop=(j == SUB - 1))
                mm.then_inc(summed, 1)

            def ahead(k, p):
                c, w = pair_at(pe, b, k)
                if pair_dots:
                    mix(k, p, c, w)
                return c, w

            pe.wait_ge(cleared, 1)

            def first():
                for k in (0, 1):
                    c, w = ahead(k, k)
                    if k == 1:
                        pe.wait_ge(low_ready, 1)
                    turn(k, k, c, w)
                spread(0, 0)
                to_edges(0, 0)
                c, w = ahead(2, 0)
                spread(1, 1)
                to_edges(1, 1)
                turn(2, 0, c, w)
                scatter(0, 0)

            def step(k, p):
                c, w = ahead(k + 2, p)
                spread(k + 1, 1 - p)
                to_edges(k + 1, 1 - p)
                turn(k + 2, p, c, w)
                scatter(k, p)

            run_pairs(pe, first, step)

        @block.scalar
        def _(act):
            def high(k, p):
                act.wait_ge(scores_turned, k + 1)
                act.activation(score_rows[0:heads, p, :], ps_t[:], ACT.Copy).then_inc(high_ready, 1)

            def shrinks(k, p):
                act.wait_ge(node_ready, k + 1)
                act.activation(shrink[:, p, :], drop[:, p, :], ACT.Exp).then_inc(shrink_ready, 1)

            def exps(k, p):
                act.wait_ge(arg_ready, k + 1)
                act.activation(ex[:, p, :, :], arg2[:, p, :, :], ACT.Exp).then_inc(ex_ready, 1)

            def first():
                for k in (0, 1):
                    high(k, k)
                shrinks(0, 0)
                exps(0, 0)
                shrinks(1, 1)
                high(2, 0)

            def step(k, p):
                exps(k, p)
                shrinks(k + 1, 1 - p)
                high(k + 2, p)

            act.wait_ge(cleared, 1)
            run_pairs(act, first, step)

        @block.vector
        def _(dve):
            def hits(k, p, c, w):
                dve.wait_ge(dst_ready, c + 1)
                dve.tensor_scalar(st[:, p, :], dst_b[:, bass.ds(c & (RING - 1), 1), :].rearrange("p t e -> p (t e)"),
                                  b.node_id[:, bass.ds(w, 1)], None, ALU.is_equal).then_inc(st_ready, 1)
                dve.wait_ge(st_ready, k + 1)
                dve.tensor_scalar(out_of[:, p, :], st[:, p, :], 1.0, -NEVER, ALU.subtract, ALU.mult)

            def mix_add(k, p, c, w):
                dve.wait_ge(mix_summed, k + 1)
                dve.wait_ge(g_ready, c + 1)
                row = g[:, bass.ds(c & (RING - 1), 1), :, :].rearrange("p t j d -> p (t j) d")
                dve.tensor_tensor(mixed[:, p, :, :], ps_x[:], row[:, :, 0:D], ALU.add)
                dve.tensor_tensor(alpha[:, p, :, :], row[:, :, D:D + heads],
                                  b.edge_logw[:, bass.ds(c, 1), :].rearrange("p t j -> p (t j)").unsqueeze(
                                      2).to_broadcast([P, SUB, heads]), ALU.add)
                dve.drain()

            def mix_dot(k, p, c, w):
                dve.scalar_tensor_tensor(mixed[:, p, :, :], mixed[:, p, :, :], 0.0,
                                         att[:].unsqueeze(1).to_broadcast([P, SUB, D]), ALU.max, ALU.mult)
                dve.drain()
                dve.tensor_reduce(bent[:, p, :, :], mixed[:, p, :, :].rearrange("p j (h c) -> p (j h) c", c=width),
                                  AX, ALU.add)
                dve.drain()
                dve.tensor_tensor(alpha[:, p, :, :], alpha[:, p, :, :], bent[:, p, :, :],
                                  ALU.add).then_inc(alpha_ready, 1)

            def low(k, p):
                dve.wait_ge(high_ready, k + 1)
                dve.tensor_tensor(score_rows[32:32 + heads, p, :], ps_t[:], score_rows[0:heads, p, :],
                                  ALU.subtract).then_inc(low_ready, 1)

            def maxima(k, p, c, w):
                for h in range(heads):
                    dve.wait_ge(spread_ready, k * heads + h + 1)
                    dve.sem_inc(held, 1)
                    dve.tensor_tensor_reduce(masked[:, (p * heads + h) % 2, :], ps_v[:, (p * heads + h) % 2, :], out_of[:, p, :], 1.0,
                                             NEVER, ALU.add, ALU.max, top[:, p, h:h + 1]).then_inc(spread_free, 1)
                dve.drain()
                now = best[:, bass.ds(w, 1), :].rearrange("p t h -> p (t h)")
                own = dst_part[:, bass.ds(w, 1), :].rearrange("p t h -> p (t h)")
                dve.tensor_tensor(cand[:, p, :], top[:, p, :], own, ALU.add)
                dve.tensor_copy(node_side[:, p, 0:heads], own)
                dve.drain()
                z = cand[:, p, :]
                if not pair_dots:
                    z = top[:, p, :]
                    dve.scalar_tensor_tensor(z, cand[:, p, :], SLOPE, cand[:, p, :], ALU.mult, ALU.max)
                    dve.drain()
                dve.tensor_tensor(node_side[:, p, heads:2 * heads], now, z, ALU.max)
                dve.drain()
                dve.tensor_tensor(drop[:, p, :], now, node_side[:, p, heads:2 * heads], ALU.subtract)
                dve.drain()
                dve.tensor_copy(now, node_side[:, p, heads:2 * heads]).then_inc(node_ready, 1)

            def args(k, p, c, w):
                dve.wait_ge(edge_ready, k + 1)
                dve.tensor_tensor(arg2[:, p, :, :], alpha[:, p, :, :], ps_m[:, :, 0:heads], ALU.add)
                dve.drain()
                score = arg2
                if not pair_dots:
                    score = arg
                    dve.scalar_tensor_tensor(arg[:, p, :, :], arg2[:, p, :, :], SLOPE, arg2[:, p, :, :],
                                             ALU.mult, ALU.max)
                    dve.drain()
                dve.tensor_tensor(arg[:, p, :, :], score[:, p, :, :], ps_m[:, :, heads:2 * heads], ALU.subtract)
                dve.drain()
                dve.tensor_scalar(arg2[:, p, :, :], arg[:, p, :, :], 30.0, None, ALU.min).then_inc(arg_ready, 1)

            def weigh(k, p, c, w):
                dve.tensor_tensor(s[:, p, :, :],
                                  b.node_iota[:, bass.ds(w * P, P)].unsqueeze(1).to_broadcast([P, SUB, P]),
                                  b.dst_id[:, bass.ds(c, 1), :].rearrange("p t j -> p (t j)").unsqueeze(
                                      2).to_broadcast([P, SUB, P]), ALU.is_equal)
                dve.wait_ge(shrink_ready, k + 1)
                dve.tensor_copy(shrink_kept[:, p, :], shrink[:, p, :])
                dve.wait_ge(ex_ready, k + 1)
                weight = ex
                if use_dist:
                    dve.tensor_tensor(exd[:, p, :, :], ex[:, p, :, :],
                                      b.edge_dist[:, bass.ds(c, 1), :].rearrange("p t j -> p (t j)").unsqueeze(
                                          2).to_broadcast([P, SUB, heads]), ALU.mult)
                    dve.drain()
                    weight = exd
                dve.tensor_copy(rows[:, p, :, :, width], ex[:, p, :, :])
                for j in range(SUB):
                    ins = dve.tensor_tensor(
                        rows[:, p, j, :, 0:width],
                        g[:, bass.ds(c & (RING - 1), 1), j, 0:D].rearrange("p t (h c) -> p (t h) c", c=width),
                        weight[:, p, j, :].unsqueeze(2).to_broadcast([P, heads, width]), ALU.mult)
                dve.drain()
                dve.sem_inc(b_done, 1)

            def add_up(k, p, w):
                dve.wait_ge(summed, k + 1)
                own = acc[:, bass.ds(w, 1), :, :].rearrange("p t h c -> p (t h) c")
                dve.tensor_tensor(own, own, shrink_kept[:, p, :].unsqueeze(2).to_broadcast([P, heads, group]), ALU.mult)
                dve.drain()
                dve.tensor_tensor(own, own, ps_o[:, p, 0:heads * group].rearrange("p (h c) -> p h c", c=group), ALU.add)
                dve.drain()

            dve.sem_inc(b_done, 1)
            dve.sem_inc(spread_free, 2)
            dve.memset(score_rows[:], 0.0)
            dve.drain()
            dve.sem_inc(cleared, 1)

            def scores(k, p):
                c, w = pair_at(dve, b, k)
                hits(k, p, c, w)
                if pair_dots:
                    mix_add(k, p, c, w)
                else:
                    dve.wait_ge(g_ready, c + 1)
                    dve.tensor_copy(alpha[:, p, :, :], g[:, bass.ds(c & (RING - 1), 1), :, D:D + heads].rearrange(
                        "p t j h -> p (t j) h")).then_inc(alpha_ready, 1)
                return c, w

            def first():
                for k in (0, 1):
                    c, w = scores(k, k)
                    if pair_dots:
                        mix_dot(k, k, c, w)
                    low(k, k)
                c, w = pair_at(dve, b, 0)
                maxima(0, 0, c, w)
                args(0, 0, c, w)
                c2, w2 = scores(2, 0)
                c1, w1 = pair_at(dve, b, 1)
                maxima(1, 1, c1, w1)
                if pair_dots:
                    mix_dot(2, 0, c2, w2)
                weigh(0, 0, c, w)
                low(2, 0)

            def step(k, p):
                c, w = pair_at(dve, b, k)
                args(k, p, c, w)
                c2, w2 = scores(k + 2, p)
                c1, w1 = pair_at(dve, b, k + 1)
                maxima(k + 1, 1 - p, c1, w1)
                if pair_dots:
                    mix_dot(k + 2, p, c2, w2)
                c0, w0 = pair_at(dve, b, k - 1)
                add_up(k - 1, 1 - p, w0)
                weigh(k, p, c, w)
                low(k + 2, p)

            half = run_pairs(dve, first, step)
            c, w = pair_at(dve, b, half * 2)
            add_up(half * 2, 0, w)


def close_first(nc, b, acc):
    heads, group = acc.shape[2], acc.shape[3]
    width = group - 1
    with Phase(nc) as ctx:
        inv = ctx.enter_context(nc.sbuf_tensor("g0_inv", [P, TILES, heads], F32))
        block = ctx.enter_context(nc.Block())

        @block.vector
        def _(dve):
            dve.tensor_scalar(inv[:], acc[:, :, :, width], 1e-30, None, ALU.max)
            dve.drain()
            dve.reciprocal(inv[:], inv[:])
            dve.drain()
            with dve.Fori(0, TILES) as t:
                own = acc[:, bass.ds(t, 1), :, 0:width].rearrange("p t h c -> p (t h) c")
                dve.tensor_tensor(own, own, inv[:, bass.ds(t, 1), :].rearrange("p t h -> p (t h)").unsqueeze(
                    2).to_broadcast([P, heads, width]), ALU.mult)
                dve.drain()
                row = b.x[:, bass.ds(t, 1), :].rearrange("p t (h c) -> p (t h) c", c=width)
                dve.tensor_tensor(row, row, own, ALU.add)


def store_stream(nc, b, out):
    with Phase(nc) as ctx:
        stored = ctx.semaphore("stored")
        block = ctx.enter_context(nc.Block())

        @block.sync
        def _(sp):
            sp.dma_start(out[0:(TILES - 1) * P, :].rearrange("(t p) d -> p t d", p=P),
                         b.x[:, 0:TILES - 1, :]).then_inc(stored, 16)
            sp.dma_start(out[(TILES - 1) * P:NODES, :], b.x[0:LAST, TILES - 1, :]).then_inc(stored, 16)
            sp.wait_ge(stored, 32)


def route(nc, b, name, experts, kind, router, router_bias, out_bias, base, total, gates, columns, first=None):
    with Phase(nc) as ctx:
        def sb(nm, shape, dt=F32):
            return ctx.enter_context(nc.sbuf_tensor(f"{name}_{nm}", shape, dt))

        def sem(nm):
            return ctx.semaphore(f"{name}_{nm}")

        rk = router.shape[0] // P
        rw = sb("rw", [P, rk, experts])
        rb = sb("rb", [P, experts])
        ob = sb("ob", [experts, D])
        logits = sb("logits", [P, TILES, experts])
        work = sb("work", [P, TILES, experts])
        picked = sb("picked", [P, TILES, experts])
        slot_id = sb("slot_id", [P, experts])
        big = sb("big", [P, TILES, 8])
        gates_t = sb("gates_t", [experts, ROWS])
        row_sets = []
        for n, (dest, recipe, arrays) in enumerate(columns):
            rows = [sb(f"rows{n}_{m}", [arrays[0].shape[0], P]) for m in range(len(arrays))]
            row_sets.append((dest, recipe, arrays, rows))
        if first:
            fw = sb("fw", [P, KD, P])
            fb = sb("fb", [P, 1])
            hidden_t = sb("hidden_t", [P, ROWS])
        ps_l = ctx.enter_context(nc.psum_tensor(f"{name}_ps_l", [P, 512], F32))
        ps_c = ctx.enter_context(nc.psum_tensor(f"{name}_ps_c", [P, 4, P], F32))
        ps_g = ctx.enter_context(nc.psum_tensor(f"{name}_ps_g", [P, 2, 512], F32))
        ps_o = ctx.enter_context(nc.psum_tensor(f"{name}_ps_o", [P, 2, 512], F32))
        ps_h = ctx.enter_context(nc.psum_tensor(f"{name}_ps_h", [P, 2, 512], F32))
        loaded = sem("loaded")
        rows_ready = sem("rows_ready")
        rows_turned = sem("rows_turned")
        rows_kept = sem("rows_kept")
        hidden_summed = sem("hidden_summed")
        hidden_ready = sem("hidden_ready")
        logits_summed = sem("logits_summed")
        diff_ready = sem("diff_ready")
        exp_ready = sem("exp_ready")
        iota_done = sem("iota_done")
        gates_ready = sem("gates_ready")
        gates_turned = sem("gates_turned")
        gates_kept = sem("gates_kept")
        out_summed = sem("out_summed")
        out_kept = sem("out_kept")
        loads = 3 + sum(len(a) for _, _, a, _ in row_sets) + (2 if first else 0)
        groups = [(c, min(512, ROWS - c)) for c in range(0, ROWS, 512)]
        block = ctx.enter_context(nc.Block())

        @block.sync
        def _(sp):
            sp.dma_start(rw[:], router.rearrange("(k p) e -> p k e", p=P)).then_inc(loaded, 16)
            sp.dma_start(rb[:], router_bias.partition_broadcast(P)).then_inc(loaded, 16)
            sp.dma_start(ob[:], out_bias).then_inc(loaded, 16)
            for _, _, arrays, rows in row_sets:
                for a, r in zip(arrays, rows):
                    sp.dma_start(r[:], a).then_inc(loaded, 16)
            if first:
                sp.dma_start(fw[:], first[0].rearrange("(k p) e -> p k e", p=P)).then_inc(loaded, 16)
                with nc.allow_non_contiguous_dma(reason="one bias column of 128 values"):
                    sp.dma_start(fb[:], first[1].rearrange("(p a) -> p a", a=1)).then_inc(loaded, 16)

        @block.gpsimd
        def _(pool):
            pool.iota(slot_id[:], [[1, experts]], base=-64, channel_multiplier=0,
                      allow_small_or_imprecise_dtypes=True).then_inc(iota_done, 1)

        @block.tensor
        def _(pe):
            pe.wait_ge(loaded, 16 * loads)
            if first:
                for n, (c, size) in enumerate(groups):
                    if n >= 2:
                        pe.wait_ge(hidden_ready, n - 1)
                    for k in range(KD):
                        mm = pe.matmul(ps_h[:, n % 2, 0:size], fw[:, k, :], b.xnT[:, k, c:c + size],
                                       start=(k == 0), stop=(k == KD - 1))
                    mm.then_inc(hidden_summed, 1)
                pe.wait_ge(hidden_ready, len(groups))
            for t in range(TILES):
                for k in range(rk):
                    a = hidden_t[:, t * P:(t + 1) * P] if first else b.xnT[:, k, t * P:(t + 1) * P]
                    mm = pe.matmul(ps_l[:, t * experts:(t + 1) * experts], a, rw[:, k, :],
                                   start=(k == 0), stop=(k == rk - 1))
            mm.then_inc(logits_summed, 1)
            n = 0
            for dest, recipe, arrays, rows in row_sets:
                for m in range(1 if recipe == "copy" else 2):
                    pe.wait_ge(rows_ready, 1)
                    if n:
                        pe.wait_ge(rows_kept, n)
                    count = rows[m].shape[0]
                    pe.transpose(ps_c[:, 0, 0:count], rows[m][:], b.ident[0:count, 0:count]).then_inc(rows_turned, 1)
                    n += 1
            pe.wait_ge(gates_ready, 1)
            for t in range(TILES):
                if t >= 2:
                    pe.wait_ge(gates_kept, t - 1)
                pe.transpose(ps_g[0:experts, t % 2, 0:P], gates[:, t, :], b.ident[:]).then_inc(gates_turned, 1)
            for t in range(TILES):
                pe.wait_ge(gates_kept, t + 1)
                if t >= 2:
                    pe.wait_ge(out_kept, t - 1)
                pe.matmul(ps_o[:, t % 2, 0:D], gates_t[:, t * P:(t + 1) * P], ob[:],
                          start=True, stop=True).then_inc(out_summed, 1)

        @block.scalar
        def _(act):
            act.wait_ge(loaded, 16 * loads)
            if first:
                for n, (c, size) in enumerate(groups):
                    act.wait_ge(hidden_summed, n + 1)
                    act.activation(hidden_t[:, c:c + size], ps_h[:, n % 2, 0:size], ACT.Relu,
                                   bias=fb[:, 0:1]).then_inc(hidden_ready, 1)
            for n in range(sum(2 for c in columns if c[1] == "norm") // 2):
                act.wait_ge(diff_ready, n + 1)
                rows = [r for r in row_sets if r[1] == "norm"][n][3]
                act.activation(rows[3][:], rows[3][:], ACT.Sqrt).then_inc(exp_ready, 1)
            base_diff = sum(1 for c in columns if c[1] == "norm")
            for n in range(2 if kind == "top2 of softmax" else 1):
                act.wait_ge(diff_ready, base_diff + n + 1)
                act.activation(work[:], work[:], ACT.Exp).then_inc(exp_ready, 1)
            for t in range(TILES):
                act.wait_ge(gates_turned, t + 1)
                act.activation(gates_t[:, t * P:(t + 1) * P], ps_g[0:experts, t % 2, 0:P],
                               ACT.Identity).then_inc(gates_kept, 1)

        @block.vector
        def _(dve):
            def wide(a):
                return a.unsqueeze(2).to_broadcast([P, TILES, experts])

            def slots():
                return slot_id[:].unsqueeze(1).to_broadcast([P, TILES, experts])

            dve.wait_ge(loaded, 16 * loads)
            steps = 0
            for dest, recipe, arrays, rows in row_sets:
                if recipe != "norm":
                    continue
                gain, offset, mean, var, bias = rows
                dve.tensor_scalar(var[:], var[:], 1e-3, None, ALU.add)
                dve.drain()
                steps += 1
                dve.sem_inc(diff_ready, 1)
                dve.wait_ge(exp_ready, steps)
                dve.reciprocal(var[:], var[:])
                dve.tensor_tensor(bias[:], bias[:], mean[:], ALU.subtract)
                dve.drain()
                dve.tensor_tensor(gain[:], gain[:], var[:], ALU.mult)
                dve.drain()
                dve.tensor_tensor(bias[:], bias[:], gain[:], ALU.mult)
                dve.drain()
                dve.tensor_tensor(offset[:], offset[:], bias[:], ALU.add)
                dve.drain()
            dve.sem_inc(rows_ready, 1)
            n = 0
            for dest, recipe, arrays, rows in row_sets:
                for m in range(1 if recipe == "copy" else 2):
                    n += 1
                    dve.wait_ge(rows_turned, n)
                    target = dest if recipe == "copy" else dest[m]
                    dve.tensor_copy(target, ps_c[:, 0, 0:rows[m].shape[0]]).then_inc(rows_kept, 1)
            dve.wait_ge(logits_summed, 1)
            dve.wait_ge(iota_done, 1)
            dve.tensor_tensor(logits[:], ps_l[:, 0:TILES * experts].rearrange("p (t e) -> p t e", e=experts),
                              rb[:].unsqueeze(1).to_broadcast([P, TILES, experts]), ALU.add)
            dve.drain()

            def softmax_all(dest):
                nonlocal steps
                dve.tensor_reduce(big[:, :, 0], logits[:], AX, ALU.max)
                dve.drain()
                dve.tensor_tensor(work[:], logits[:], wide(big[:, :, 0]), ALU.subtract)
                dve.drain()
                steps += 1
                dve.sem_inc(diff_ready, 1)
                dve.wait_ge(exp_ready, steps)
                dve.tensor_reduce(big[:, :, 1], work[:], AX, ALU.add)
                dve.drain()
                dve.reciprocal(big[:, :, 2], big[:, :, 1])
                dve.drain()
                dve.tensor_tensor(dest, work[:], wide(big[:, :, 2]), ALU.mult)
                dve.drain()

            def largest(value, chosen):
                dve.tensor_reduce(value, logits[:], AX, ALU.max)
                dve.drain()
                dve.tensor_tensor(chosen, logits[:], wide(value), ALU.is_equal)
                dve.drain()
                dve.tensor_tensor(chosen, chosen, slots(), ALU.mult)
                dve.drain()
                dve.tensor_reduce(big[:, :, 7], chosen, AX, ALU.min)
                dve.drain()
                dve.tensor_tensor(chosen, slots(), wide(big[:, :, 7]), ALU.is_equal)
                dve.drain()

            if kind == "all":
                softmax_all(gates[:])
            else:
                if kind == "top2 of softmax":
                    softmax_all(logits[:])
                largest(big[:, :, 3], gates[:])
                dve.scalar_tensor_tensor(logits[:], gates[:], NEVER, logits[:], ALU.mult, ALU.add)
                dve.drain()
                largest(big[:, :, 4], picked[:])
                dve.tensor_tensor(work[:], wide(big[:, :, 4]), wide(big[:, :, 3]), ALU.subtract)
                dve.drain()
                steps += 1
                dve.sem_inc(diff_ready, 1)
                dve.wait_ge(exp_ready, steps)
                dve.tensor_scalar(big[:, :, 5], work[:, :, 0], 1.0, None, ALU.add)
                dve.tensor_tensor(picked[:], picked[:], work[:], ALU.mult)
                dve.drain()
                dve.reciprocal(big[:, :, 6], big[:, :, 5])
                dve.tensor_tensor(gates[:], gates[:], picked[:], ALU.add)
                dve.drain()
                dve.tensor_tensor(gates[:], gates[:], wide(big[:, :, 6]), ALU.mult)
                dve.drain()
            dve.sem_inc(gates_ready, 1)
            for t in range(TILES):
                dve.wait_ge(out_summed, t + 1)
                dve.tensor_tensor(total[:, t, :], base[:, t, :], ps_o[:, t % 2, 0:D], ALU.add).then_inc(out_kept, 1)


def run_experts(nc, b, name, experts, mats, columns, gates, total):
    hidden = len(mats) - 1
    groups = [(c, min(512, ROWS - c)) for c in range(0, ROWS, 512)]
    H_BANKS, O_BANKS = 4, 2
    with Phase(nc) as ctx:
        def sb(nm, shape, dt=F32):
            return ctx.enter_context(nc.sbuf_tensor(f"{name}_{nm}", shape, dt))

        def sem(nm):
            return ctx.semaphore(f"{name}_{nm}")

        w, h, now = [], [], []
        for i, m in enumerate(mats):
            rows, cols = m.shape[1], m.shape[2]
            w.append(sb(f"w{i}", [P, 2, rows // P, cols]))
            if i < hidden:
                h.append(sb(f"h{i}", [P, 2, cols // P, 512]))
                now.append(sb(f"now{i}", [P, 2, 2, cols // P]))
        ps_h = ctx.enter_context(nc.psum_tensor(f"{name}_ps_h", [P, H_BANKS, 512], F32))
        ps_o = ctx.enter_context(nc.psum_tensor(f"{name}_ps_o", [P, O_BANKS, 512], F32))
        landed = [sem("landed0"), sem("landed1")]
        expert_done = sem("expert_done")
        hidden_summed = sem("hidden_summed")
        hidden_kept = sem("hidden_kept")
        out_summed = sem("out_summed")
        out_kept = sem("out_kept")
        tiles_f = [m.shape[2] // P for m in mats[:hidden]]
        per_expert = len(groups) * sum(tiles_f)

        order = [(i, q - i) for q in range(len(groups) + hidden) for i in range(hidden + 1)
                 if 0 <= q - i < len(groups)]
        place, at = {}, 0
        for i, g in order:
            if i < hidden:
                place[(i, g)] = at
                at += tiles_f[i]

        block = ctx.enter_context(nc.Block())

        @block.sync
        def _(sp):
            def load(e, u):
                for i, m in enumerate(mats):
                    sp.dma_start(w[i][:, u, :, :], m[bass.ds(e, 1), :, :].rearrange(
                        "x (k p) n -> p (x k) n", p=P)).then_inc(landed[u], 16)

            load(0, 0)
            load(1, 1)
            with sp.Fori(1, experts // 2) as j:
                for u in range(2):
                    sp.wait_ge(expert_done, j * 2 + u - 1)
                    load(j * 2 + u, u)

        @block.tensor
        def _(pe):
            with pe.Fori(0, experts // 2) as j:
                for u in range(2):
                    e = j * 2 + u
                    pe.wait_ge(landed[u], (j + 1) * (16 * len(mats)))
                    for i, g in order:
                        start_col, size = groups[g]
                        src = b.xnT if i == 0 else h[i - 1]
                        par = g % 2
                        ks = mats[i].shape[1] // P
                        if i:
                            pe.wait_ge(hidden_kept, e * per_expert + (H_BANKS + place[(i - 1, g)] + tiles_f[i - 1]))
                        if i < hidden:
                            for f in range(tiles_f[i]):
                                n = place[(i, g)] + f
                                bank = (u * per_expert + n) % H_BANKS
                                pe.wait_ge(hidden_kept, e * per_expert + (n + 1))
                                for k in range(ks):
                                    a = (src[:, k, start_col:start_col + size] if i == 0
                                         else src[:, par, k, 0:size])
                                    mm = pe.matmul(ps_h[:, bank, 0:size], w[i][:, u, k, f * P:(f + 1) * P], a,
                                                   start=(k == 0), stop=(k == ks - 1))
                                mm.then_inc(hidden_summed, 1)
                        else:
                            for s in range(size // P):
                                t = start_col // P + s
                                bank = (u * TILES + t) % O_BANKS
                                pe.wait_ge(out_kept, e * TILES + (t + 1))
                                for k in range(ks):
                                    mm = pe.matmul(ps_o[:, bank, 0:D], src[:, par, k, s * P:(s + 1) * P],
                                                   w[i][:, u, k, :], start=(k == 0), stop=(k == ks - 1))
                                mm.then_inc(out_summed, 1)
                    pe.wait_ge(out_summed, e * TILES + TILES)
                    pe.sem_inc(expert_done, 1)

        @block.scalar
        def _(act):
            act.sem_inc(hidden_kept, H_BANKS)
            with act.Fori(0, experts // 2) as j:
                for u in range(2):
                    e = j * 2 + u
                    for i in range(hidden):
                        for m, col in enumerate(columns[i]):
                            if col is not None:
                                act.activation(now[i][:, u, m, :], col[:, bass.ds(e * tiles_f[i], tiles_f[i])],
                                               ACT.Identity)
                    act.drain()
                    for i, g in order:
                        if i == hidden:
                            continue
                        size = groups[g][1]
                        scaled = columns[i][0] is not None
                        for f in range(tiles_f[i]):
                            n = place[(i, g)] + f
                            bank = (u * per_expert + n) % H_BANKS
                            act.wait_ge(hidden_summed, e * per_expert + (n + 1))
                            act.activation(h[i][:, g % 2, f, 0:size], ps_h[:, bank, 0:size], ACT.Relu,
                                           bias=now[i][:, u, 1, f:f + 1],
                                           scale=now[i][:, u, 0, f:f + 1] if scaled else 1.0).then_inc(hidden_kept, 1)

        @block.vector
        def _(dve):
            dve.sem_inc(out_kept, O_BANKS)
            with dve.Fori(0, experts // 2) as j:
                for u in range(2):
                    e = j * 2 + u
                    for t in range(TILES):
                        dve.wait_ge(out_summed, e * TILES + (t + 1))
                        dve.scalar_tensor_tensor(total[:, t, :], ps_o[:, (u * TILES + t) % O_BANKS, 0:D],
                                                 gates[:, t, bass.ds(e, 1)], total[:, t, :],
                                                 ALU.mult, ALU.add).then_inc(out_kept, 1)
                    dve.drain()


def close_moe(nc, b, y, gamma, beta):
    with Phase(nc) as ctx:
        def sb(nm, shape, dt=F32):
            return ctx.enter_context(nc.sbuf_tensor(f"moe_{nm}", shape, dt))

        def sem(nm):
            return ctx.semaphore(f"moe_{nm}")

        gain = sb("gain", [P, D])
        bias = sb("bias", [P, D])
        stats = sb("stats", [P, TILES, 6])
        moments = sb("moments", [P, TILES, 2])
        spread = sb("spread", [P, TILES])
        loaded = sem("loaded")
        spread_ready = sem("spread_ready")
        rooted = sem("rooted")
        block = ctx.enter_context(nc.Block())

        @block.sync
        def _(sp):
            sp.dma_start(gain[:], gamma.partition_broadcast(P)).then_inc(loaded, 16)
            sp.dma_start(bias[:], beta.partition_broadcast(P)).then_inc(loaded, 16)

        @block.scalar
        def _(act):
            act.wait_ge(spread_ready, 1)
            act.activation(spread[:], spread[:], ACT.Sqrt).then_inc(rooted, 1)

        @block.vector
        def _(dve):
            with dve.Fori(0, TILES) as t:
                dve.bn_stats(stats[:, bass.ds(t, 1), :].rearrange("p t s -> p (t s)"),
                             y[:, bass.ds(t, 1), :].rearrange("p t d -> p (t d)"))
            dve.drain()
            for t in range(TILES):
                dve.bn_aggr(moments[:, t, :], stats[:, t, :])
            dve.drain()
            dve.tensor_scalar(spread[:], moments[:, :, 1], 1e-5, None, ALU.add).then_inc(spread_ready, 1)
            dve.wait_ge(rooted, 1)
            dve.reciprocal(spread[:], spread[:])
            dve.wait_ge(loaded, 32)
            dve.drain()
            with dve.Fori(0, TILES) as t:
                row = y[:, bass.ds(t, 1), :].rearrange("p t d -> p (t d)")
                x = b.x[:, bass.ds(t, 1), :].rearrange("p t d -> p (t d)")
                dve.tensor_scalar(row, row, moments[:, bass.ds(t, 1), 0], spread[:, bass.ds(t, 1)],
                                  ALU.subtract, ALU.mult)
                dve.drain()
                dve.tensor_tensor(row, row, gain[:], ALU.mult)
                dve.tensor_tensor(x, x, bias[:], ALU.add)
                dve.drain()
                dve.tensor_tensor(x, x, row, ALU.add)


def over_denominators(nc, b, name, acc, h, bias, floor, elu):
    heads, group = acc.shape[2], acc.shape[3]
    width = group - 1
    with Phase(nc) as ctx:
        def sb(nm, shape, dt=F32):
            return ctx.enter_context(nc.sbuf_tensor(f"{name}_{nm}", shape, dt))

        def sem(nm):
            return ctx.semaphore(f"{name}_{nm}")

        inv = sb("inv", [P, TILES, heads])
        bias_b = sb("bias_b", [P, D])
        low = sb("low", [P, 2, D])
        loaded = sem("loaded")
        low_ready = sem("low_ready")
        low_exp = sem("low_exp")
        block = ctx.enter_context(nc.Block())

        @block.sync
        def _(sp):
            sp.dma_start(bias_b[:], bias.partition_broadcast(P)).then_inc(loaded, 16)

        if elu:
            @block.scalar
            def _(act):
                for t in range(TILES):
                    act.wait_ge(low_ready, t + 1)
                    act.activation(low[:, t % 2, :], low[:, t % 2, :], ACT.Exp).then_inc(low_exp, 1)

        @block.vector
        def _(dve):
            dve.tensor_scalar(inv[:], acc[:, :, :, width], floor, None, ALU.add)
            dve.drain()
            dve.reciprocal(inv[:], inv[:])
            dve.wait_ge(loaded, 16)
            dve.drain()

            def upper(t):
                row = h[:, t, :]
                dve.wait_ge(low_exp, t + 1)
                dve.tensor_scalar(row, row, 0.0, -1.0, ALU.max, ALU.add)
                dve.drain()
                dve.tensor_tensor(row, row, low[:, t % 2, :], ALU.add)

            for t in range(TILES):
                row = h[:, t, :]
                dve.tensor_tensor(row.rearrange("p (h c) -> p h c", c=width), acc[:, t, :, 0:width],
                                  inv[:, t, :].unsqueeze(2).to_broadcast([P, heads, width]), ALU.mult)
                dve.drain()
                dve.tensor_tensor(row, row, bias_b[:], ALU.add)
                dve.drain()
                if elu:
                    dve.tensor_scalar(low[:, t % 2, :], row, 0.0, None, ALU.min).then_inc(low_ready, 1)
                    if t:
                        upper(t - 1)
            if elu:
                upper(TILES - 1)


def turn_tiles(nc, b, name, h):
    with Phase(nc) as ctx:
        ps_t = ctx.enter_context(nc.psum_tensor(f"{name}_ps_t", [P, BANKS, 2, KD, P], F32))
        tile_turned = ctx.semaphore(f"{name}_tile_turned")
        bank_free = ctx.semaphore(f"{name}_bank_free")
        block = ctx.enter_context(nc.Block())

        @block.scalar
        def _(act):
            act.sem_inc(bank_free, BANKS)
            with act.Fori(0, TILES // BANKS) as i:
                for u in range(BANKS):
                    t = i * BANKS + u
                    act.wait_ge(tile_turned, t + 1)
                    act.activation(b.xnT[:, :, bass.ds(t * P, P)], ps_t[:, u, 0, :, :],
                                   ACT.Identity).then_inc(bank_free, 1)

        @block.tensor
        def _(pe):
            for t in range(TILES):
                pe.wait_ge(bank_free, t + 1)
                for k in range(KD):
                    mm = pe.transpose(ps_t[:, t % BANKS, 0, k, :], h[:, t, k * P:(k + 1) * P], b.ident[:])
                mm.then_inc(tile_turned, 1)


def close_gat(nc, b, h, vectors):
    with Phase(nc) as ctx:
        def sb(nm, shape, dt=F32):
            return ctx.enter_context(nc.sbuf_tensor(f"gat_{nm}", shape, dt))

        def sem(nm):
            return ctx.semaphore(f"gat_{nm}")

        v = [sb(f"v{i}", [P, D]) for i in range(len(vectors))]
        gain, offset, mean, var, ln_gain, ln_bias = v
        stats = sb("stats", [P, TILES, 6])
        moments = sb("moments", [P, TILES, 2])
        spread = sb("spread", [P, TILES])
        loaded = sem("loaded")
        root_asked = sem("root_asked")
        rooted = sem("rooted")
        block = ctx.enter_context(nc.Block())

        @block.sync
        def _(sp):
            for tile, a in zip(v, vectors):
                sp.dma_start(tile[:], a.partition_broadcast(P)).then_inc(loaded, 16)

        @block.scalar
        def _(act):
            act.wait_ge(root_asked, 1)
            act.activation(var[:], var[:], ACT.Sqrt).then_inc(rooted, 1)
            act.wait_ge(root_asked, 2)
            act.activation(spread[:], spread[:], ACT.Sqrt).then_inc(rooted, 1)

        @block.vector
        def _(dve):
            dve.wait_ge(loaded, 16 * len(vectors))
            dve.tensor_scalar(var[:], var[:], 1e-5, None, ALU.add).then_inc(root_asked, 1)
            dve.wait_ge(rooted, 1)
            dve.reciprocal(var[:], var[:])
            dve.drain()
            dve.tensor_tensor(gain[:], gain[:], var[:], ALU.mult)
            dve.drain()
            dve.tensor_tensor(mean[:], mean[:], gain[:], ALU.mult)
            dve.drain()
            dve.tensor_tensor(offset[:], offset[:], mean[:], ALU.subtract)
            dve.drain()
            for t in range(TILES):
                dve.tensor_tensor(h[:, t, :], h[:, t, :], gain[:], ALU.mult)
                if t:
                    dve.tensor_tensor(h[:, t - 1, :], h[:, t - 1, :], offset[:], ALU.add)
                dve.drain()
            dve.tensor_tensor(h[:, TILES - 1, :], h[:, TILES - 1, :], offset[:], ALU.add)
            dve.drain()
            for t in range(TILES):
                dve.bn_stats(stats[:, t, :], h[:, t, :])
            dve.drain()
            for t in range(TILES):
                dve.bn_aggr(moments[:, t, :], stats[:, t, :])
            dve.drain()
            dve.tensor_scalar(spread[:], moments[:, :, 1], 1e-5, None, ALU.add).then_inc(root_asked, 1)
            dve.wait_ge(rooted, 2)
            dve.reciprocal(spread[:], spread[:])
            dve.drain()
            with dve.Fori(0, TILES) as t:
                row = h[:, bass.ds(t, 1), :].rearrange("p t d -> p (t d)")
                x = b.x[:, bass.ds(t, 1), :].rearrange("p t d -> p (t d)")
                dve.tensor_scalar(row, row, moments[:, bass.ds(t, 1), 0], spread[:, bass.ds(t, 1)],
                                  ALU.subtract, ALU.mult)
                dve.drain()
                dve.tensor_tensor(row, row, ln_gain[:], ALU.mult)
                dve.tensor_tensor(x, x, ln_bias[:], ALU.add)
                dve.drain()
                dve.tensor_tensor(x, x, row, ALU.add)


def add_to_stream(nc, b, h):
    block_ctx = nc.Block()
    with block_ctx as block:
        @block.vector
        def _(dve):
            dve.tensor_tensor(b.x[:], b.x[:], h[:], ALU.add)


def pair_tables(nc, b, name, w_l, b_l, w_r, b_r, attention, table, x_r, acc, best, dst_part, att):
    with Phase(nc) as ctx:
        def sb(nm, shape, dt=F32):
            return ctx.enter_context(nc.sbuf_tensor(f"{name}_{nm}", shape, dt))

        def sem(nm):
            return ctx.semaphore(f"{name}_{nm}")

        w = sb("w", [P, KD, 2, D])
        bias = sb("bias", [P, 2, D])
        heads = acc.shape[2]
        stage = sb("stage", [P, BANKS, D + heads])
        slope_att = sb("slope_att", [P, D])
        prod = sb("prod", [P, BANKS, 2, D])
        ps = ctx.enter_context(nc.psum_tensor(f"{name}_ps", [P, BANKS, 512], F32))
        loaded = sem("loaded")
        projected = sem("projected")
        kept = sem("kept")
        staged = sem("staged")
        stored = [sem(f"stored{u}") for u in range(BANKS)]
        block = ctx.enter_context(nc.Block())

        @block.sync
        def _(sp):
            for i, (m, v) in enumerate(((w_l, b_l), (w_r, b_r))):
                sp.dma_start(w[:, :, i, :], m.rearrange("(k p) n -> p k n", p=P)).then_inc(loaded, 16)
                sp.dma_start(bias[:, i, :], v.partition_broadcast(P)).then_inc(loaded, 16)
            sp.dma_start(att[:], attention.partition_broadcast(P)).then_inc(loaded, 16)
            for u in range(BANKS):
                sp.sem_inc(stored[u], 16)
            with sp.Fori(0, TILES // BANKS) as i:
                for u in range(BANKS):
                    t = i * BANKS + u
                    sp.wait_ge(staged, t + 1)
                    sp.dma_start(table[bass.ds(t * P, P), :], stage[:, u, :]).then_inc(stored[u], 16)
            for u in range(BANKS):
                sp.wait_ge(stored[u], 16 * (TILES // BANKS + 1))

        @block.tensor
        def _(pe):
            pe.wait_ge(loaded, 80)
            for t in range(TILES):
                pe.wait_ge(kept, t + 1)
                for k in range(KD):
                    mm = pe.matmul(ps[:, t % BANKS, :], b.xnT[:, k, t * P:(t + 1) * P],
                                   w[:, k, :, :].rearrange("p i n -> p (i n)"),
                                   start=(k == 0), stop=(k == KD - 1))
                mm.then_inc(projected, 1)

        @block.vector
        def _(dve):
            dve.sem_inc(kept, BANKS)
            dve.memset(acc[:], 0.0)
            dve.memset(best[:], NEVER)
            dve.wait_ge(loaded, 80)
            dve.tensor_scalar(slope_att[:], att[:], SLOPE, None, ALU.mult)
            dve.drain()
            dve.tensor_scalar(att[:], att[:], 1.0 - SLOPE, None, ALU.mult)
            with dve.Fori(0, TILES // BANKS) as i:
                for u in range(BANKS):
                    t = i * BANKS + u
                    dve.wait_ge(projected, t + 1)
                    dve.wait_ge(stored[u], (i + 1) * 16)
                    right = x_r[:, bass.ds(t, 1), :].rearrange("p t d -> p (t d)")
                    dve.tensor_tensor(stage[:, u, 0:D], ps[:, u, 0:D], bias[:, 0, :], ALU.add)
                    dve.tensor_tensor(right, ps[:, u, D:2 * D], bias[:, 1, :], ALU.add).then_inc(kept, 1)
                    dve.drain()
                    dve.tensor_tensor(prod[:, u, 0, :], stage[:, u, 0:D], slope_att[:], ALU.mult)
                    dve.tensor_tensor(prod[:, u, 1, :], right, slope_att[:], ALU.mult)
                    dve.drain()
                    dve.tensor_reduce(stage[:, u, D:D + heads], prod[:, u, 0, :].rearrange(
                        "p (h c) -> p h c", h=heads), AX, ALU.add).then_inc(staged, 1)
                    dve.tensor_reduce(dst_part[:, bass.ds(t, 1), :].rearrange("p t h -> p (t h)"),
                                      prod[:, u, 1, :].rearrange("p (h c) -> p h c", h=heads), AX, ALU.add)


def direction_tables(nc, b, name, h, w1, b1, table, node_side, edge_abs):
    with Phase(nc) as ctx:
        def sb(nm, shape, dt=F32):
            return ctx.enter_context(nc.sbuf_tensor(f"{name}_{nm}", shape, dt))

        def sem(nm):
            return ctx.semaphore(f"{name}_{nm}")

        w = sb("w", [P, KD, 2, D])
        bias = sb("bias", [P, D])
        stage = sb("stage", [P, BANKS, D + 1])
        stage_q = sb("stage_q", [P, BANKS, D])
        ps = ctx.enter_context(nc.psum_tensor(f"{name}_ps", [P, BANKS, 512], F32))
        loaded = sem("loaded")
        projected = sem("projected")
        kept = sem("kept")
        staged = sem("staged")
        h_stored = sem("h_stored")
        stored = [sem(f"stored{u}") for u in range(BANKS)]
        block = ctx.enter_context(nc.Block())

        @block.sync
        def _(sp):
            for i in range(2):
                sp.dma_start(w[:, :, i, :], w1[i * D:(i + 1) * D, :].rearrange(
                    "(k p) n -> p k n", p=P)).then_inc(loaded, 16)
            sp.dma_start(bias[:], b1.partition_broadcast(P)).then_inc(loaded, 16)
            sp.dma_start(node_side[:, D:2 * D].rearrange("(t p) d -> p t d", p=P), h[:]).then_inc(h_stored, 16)
            for u in range(BANKS):
                sp.sem_inc(stored[u], 32)
            with sp.Fori(0, TILES // BANKS) as i:
                for u in range(BANKS):
                    t = i * BANKS + u
                    sp.wait_ge(staged, t + 1)
                    sp.dma_start(table[bass.ds(t * P, P), :], stage[:, u, :]).then_inc(stored[u], 16)
                    sp.dma_start(node_side[bass.ds(t * P, P), 0:D], stage_q[:, u, :]).then_inc(stored[u], 16)
            for u in range(BANKS):
                sp.wait_ge(stored[u], 32 * (TILES // BANKS + 1))
            sp.wait_ge(h_stored, 16)

        @block.tensor
        def _(pe):
            pe.wait_ge(loaded, 48)
            for t in range(TILES):
                pe.wait_ge(kept, t + 1)
                for k in range(KD):
                    mm = pe.matmul(ps[:, t % BANKS, :], b.xnT[:, k, t * P:(t + 1) * P],
                                   w[:, k, :, :].rearrange("p i n -> p (i n)"),
                                   start=(k == 0), stop=(k == KD - 1))
                mm.then_inc(projected, 1)

        @block.vector
        def _(dve):
            dve.sem_inc(kept, BANKS)
            dve.memset(stage[:, :, D:D + 1], 1.0)
            dve.tensor_scalar(edge_abs[:], b.edge_dir[:], -1.0, None, ALU.mult)
            dve.drain()
            dve.tensor_tensor(edge_abs[:], edge_abs[:], b.edge_dir[:], ALU.max)
            dve.wait_ge(loaded, 48)
            with dve.Fori(0, TILES // BANKS) as i:
                for u in range(BANKS):
                    t = i * BANKS + u
                    dve.wait_ge(projected, t + 1)
                    dve.wait_ge(stored[u], (i + 1) * 32)
                    dve.tensor_copy(stage[:, u, 0:D], ps[:, u, 0:D])
                    dve.tensor_tensor(stage_q[:, u, :], ps[:, u, D:2 * D], bias[:], ALU.add)
                    dve.drain()
                    dve.sem_inc(staged, 1)
                    dve.sem_inc(kept, 1)


def direct(nc, b, name, table, acc, edge_abs):
    with Phase(nc) as ctx:
        def sb(nm, shape, dt=F32):
            return ctx.enter_context(nc.sbuf_tensor(f"{name}_{nm}", shape, dt))

        def sem(nm):
            return ctx.semaphore(f"{name}_{nm}")

        done = sem("done")
        g, dst_b, g_ready, dst_ready, pool_program, sp_program = load_chunks(nc, b, ctx, name, D + 1, done)
        s = sb("s", [P, 2, 3, SUB, P])
        ps = ctx.enter_context(nc.psum_tensor(f"{name}_ps", [P, 2, 3, 512], F32))
        hits_ready = sem("hits_ready")
        s_ready = sem("s_ready")
        block = ctx.enter_context(nc.Block())

        @block.gpsimd
        def _(pool):
            pool_program(pool, table)

        @block.tensor
        def _(pe):
            def scatter(k, p):
                c, w = pair_at(pe, b, k)
                pe.wait_ge(g_ready, c + 1)
                pe.wait_ge(s_ready, k + 1)
                for i in range(3):
                    for j in range(SUB):
                        mm = pe.matmul(ps[:, p, i, 0:D + 1], s[:, p, i, j, :],
                                       g[:, bass.ds(c & (RING - 1), 1), j, :].rearrange("p t d -> p (t d)"),
                                       start=(j == 0), stop=(j == SUB - 1))
                mm.then_inc(done, 1)

            pe.sem_inc(done, 1)
            half = pe.value_load(b.half_pairs[0:1, 0:1], min_val=1, max_val=PAIRS_MAX // 2 - 2)
            scatter(0, 0)
            with pe.Fori(0, half) as i:
                for u in (1, 2):
                    scatter(i * 2 + u, u % 2)

        @block.vector
        def _(dve):
            def weights(k, p):
                c, w = pair_at(dve, b, k)

                def wide(a):
                    return a[:, bass.ds(c, 1), :].rearrange("p t j -> p (t j)").unsqueeze(
                        2).to_broadcast([P, SUB, P])

                dve.tensor_tensor(s[:, p, 0, :, :],
                                  b.node_iota[:, bass.ds(w * P, P)].unsqueeze(1).to_broadcast([P, SUB, P]),
                                  wide(b.dst_id), ALU.is_equal).then_inc(hits_ready, 1)
                dve.wait_ge(hits_ready, k + 1)
                dve.tensor_tensor(s[:, p, 1, :, :], s[:, p, 0, :, :], wide(b.edge_dir), ALU.mult)
                dve.tensor_tensor(s[:, p, 2, :, :], s[:, p, 0, :, :], wide(edge_abs), ALU.mult)
                dve.drain()
                dve.sem_inc(s_ready, 1)

            def add_up(k, p):
                c, w = pair_at(dve, b, k)
                dve.wait_ge(done, k + 2)
                own = acc[:, bass.ds(w, 1), :, :].rearrange("p t i c -> p (t i) c")
                dve.tensor_tensor(own, own, ps[:, p, :, 0:D + 1], ALU.add)
                dve.drain()

            dve.memset(acc[:], 0.0)
            dve.drain()
            half = dve.value_load(b.half_pairs[0:1, 0:1], min_val=1, max_val=PAIRS_MAX // 2 - 2)
            weights(0, 0)
            with dve.Fori(0, half) as i:
                for u in (1, 2):
                    weights(i * 2 + u, u % 2)
                    add_up(i * 2 + u - 1, (u - 1) % 2)
            add_up(half * 2, 0)


def close_direction(nc, b, acc, node_side, w2, b2, snorm, gamma, beta):
    with Phase(nc) as ctx:
        def sb(nm, shape, dt=F32):
            return ctx.enter_context(nc.sbuf_tensor(f"dgn_{nm}", shape, dt))

        def sem(nm):
            return ctx.semaphore(f"dgn_{nm}")

        KW = 4 * KD
        w = sb("w", [P, KW, D])
        vec = sb("vec", [P, 3, D])
        snorm_rows = sb("snorm_rows", [TILES, P])
        norm = sb("norm", [P, TILES])
        side = sb("side", [P, 2, 2 * D])
        coef = sb("coef", [P, TILES, 8])
        parts = sb("parts", [P, 2, 3, D])
        parts_t = sb("parts_t", [P, 2, 3 * KD, P])
        ones = sb("ones", [P, P])
        square = sb("square", [P, 2, D])
        mean = sb("mean", [P, D])
        var = sb("var", [P, D])
        ps_t = ctx.enter_context(nc.psum_tensor("dgn_ps_t", [P, 8, P], F32))
        ps_o = ctx.enter_context(nc.psum_tensor("dgn_ps_o", [P, 2, 512], F32))
        ps_s = ctx.enter_context(nc.psum_tensor("dgn_ps_s", [P, 2, 512], F32))
        ps_n = ctx.enter_context(nc.psum_tensor("dgn_ps_n", [P, 512], F32))
        loaded = sem("loaded")
        snorm_filled = sem("snorm_filled")
        side_loaded = [sem("side_loaded0"), sem("side_loaded1")]
        norm_turned = sem("norm_turned")
        parts_ready = sem("parts_ready")
        parts_turned = sem("parts_turned")
        parts_kept = sem("parts_kept")
        out_summed = sem("out_summed")
        out_kept = sem("out_kept")
        mean_summed = sem("mean_summed")
        square_ready = sem("square_ready")
        square_summed = sem("square_summed")
        var_summed = sem("var_summed")
        root_asked = sem("root_asked")
        rooted = sem("rooted")
        out = acc[:, :, 0, 0:D]
        block = ctx.enter_context(nc.Block())

        def real(t):
            return LAST if t == TILES - 1 else P

        @block.sync
        def _(sp):
            sp.dma_start(w[:], w2.rearrange("(k p) n -> p k n", p=P)).then_inc(loaded, 16)
            for i, v in enumerate((b2, gamma, beta)):
                sp.dma_start(vec[:, i, :], v.partition_broadcast(P)).then_inc(loaded, 16)
            sp.wait_ge(snorm_filled, 1)
            sp.dma_start(snorm_rows[0:TILES - 1, :],
                         snorm[0:(TILES - 1) * P].rearrange("(t p) -> t p", p=P)).then_inc(loaded, 16)
            sp.dma_start(snorm_rows[TILES - 1:TILES, 0:LAST],
                         snorm[(TILES - 1) * P:NODES].rearrange("(t p) -> t p", t=1)).then_inc(loaded, 16)
            for t in range(TILES):
                if t >= 2:
                    sp.wait_ge(out_kept, t - 1)
                sp.dma_start(side[:, t % 2, :], node_side[t * P:(t + 1) * P, :]).then_inc(side_loaded[t % 2], 16)

        @block.gpsimd
        def _(pool):
            pool.memset(snorm_rows[:], 0.0).then_inc(snorm_filled, 1)
            pool.memset(ones[:], 1.0).then_inc(snorm_filled, 1)

        @block.tensor
        def _(pe):
            pe.wait_ge(loaded, 16 * 6)
            pe.transpose(ps_n[:, 0:TILES], snorm_rows[:], b.ident[0:TILES, 0:TILES]).then_inc(norm_turned, 1)
            for t in range(TILES):
                pe.wait_ge(parts_ready, t + 1)
                if t:
                    pe.wait_ge(parts_kept, t)
                for i in range(3):
                    for k in range(KD):
                        mm = pe.transpose(ps_t[:, i * KD + k, :], parts[:, t % 2, i, k * P:(k + 1) * P], b.ident[:])
                mm.then_inc(parts_turned, 1)
                if t >= 2:
                    pe.wait_ge(out_kept, t - 1)
                for k in range(KD):
                    pe.matmul(ps_o[:, t % 2, 0:D], b.xnT[:, k, t * P:(t + 1) * P], w[:, k, :],
                              start=(k == 0), stop=False)
                pe.wait_ge(parts_kept, t + 1)
                for k in range(3 * KD):
                    mm = pe.matmul(ps_o[:, t % 2, 0:D], parts_t[:, t % 2, k, :], w[:, KD + k, :],
                                   start=False, stop=(k == 3 * KD - 1))
                mm.then_inc(out_summed, 1)
            pe.wait_ge(snorm_filled, 2)
            for t in range(TILES):
                pe.wait_ge(out_kept, t + 1)
                mm = pe.matmul(ps_s[:, 0, 0:D], ones[0:real(t), :], out[0:real(t), t, :],
                               start=(t == 0), stop=(t == TILES - 1))
            mm.then_inc(mean_summed, 1)
            for t in range(TILES):
                pe.wait_ge(square_ready, t + 1)
                pe.matmul(ps_s[:, 1, 0:D], ones[0:real(t), :], square[0:real(t), t % 2, :],
                          start=(t == 0), stop=(t == TILES - 1)).then_inc(square_summed, 1)

        @block.scalar
        def _(act):
            for t in range(TILES):
                act.wait_ge(parts_turned, t + 1)
                act.activation(parts_t[:, t % 2, :, :], ps_t[:, 0:3 * KD, :], ACT.Identity).then_inc(parts_kept, 1)
            act.wait_ge(root_asked, 1)
            act.activation(var[:], var[:], ACT.Sqrt).then_inc(rooted, 1)

        @block.vector
        def _(dve):
            dve.wait_ge(loaded, 16 * 6)
            dve.wait_ge(norm_turned, 1)
            dve.tensor_copy(norm[:], ps_n[:, 0:TILES])
            deg, sum_w, sum_a = (acc[:, :, i, D] for i in range(3))
            dve.tensor_scalar(coef[:, :, 5], deg, 1.0, None, ALU.max)
            dve.tensor_scalar(coef[:, :, 6], sum_a, 1e-8, None, ALU.add)
            dve.drain()
            dve.reciprocal(coef[:, :, 0], coef[:, :, 5])
            dve.reciprocal(coef[:, :, 2], coef[:, :, 6])
            dve.drain()
            dve.tensor_tensor(coef[:, :, 1], coef[:, :, 0], deg, ALU.mult)
            dve.tensor_tensor(coef[:, :, 3], coef[:, :, 2], sum_a, ALU.mult)
            dve.tensor_tensor(coef[:, :, 4], coef[:, :, 2], sum_w, ALU.mult)
            dve.drain()

            def keep_out(t):
                dve.wait_ge(out_summed, t + 1)
                dve.tensor_tensor(out[:, t, :], ps_o[:, t % 2, 0:D], vec[:, 0, :], ALU.add)
                dve.drain()
                dve.tensor_scalar(out[:, t, :], out[:, t, :], norm[:, t:t + 1], None, ALU.mult).then_inc(out_kept, 1)

            for t in range(TILES):
                dve.wait_ge(side_loaded[t % 2], 16 * (t // 2 + 1))
                q, h = side[:, t % 2, 0:D], side[:, t % 2, D:2 * D]
                for i, (whole, share) in enumerate(((0, 1), (2, 3), (2, 4))):
                    dve.tensor_scalar(parts[:, t % 2, i, :], q, coef[:, t, share:share + 1], None, ALU.mult)
                dve.drain()
                for i, (source, whole) in enumerate(((0, 0), (2, 2), (1, 2))):
                    dve.scalar_tensor_tensor(parts[:, t % 2, i, :], acc[:, t, source, 0:D],
                                             coef[:, t, whole:whole + 1], parts[:, t % 2, i, :], ALU.mult, ALU.add)
                dve.drain()
                last = parts[:, t % 2, 2, :]
                dve.tensor_tensor(last, last, h, ALU.subtract)
                dve.drain()
                dve.scalar_tensor_tensor(last, last, -1.0, last, ALU.mult, ALU.max).then_inc(parts_ready, 1)
                if t:
                    keep_out(t - 1)
            keep_out(TILES - 1)
            dve.wait_ge(mean_summed, 1)
            dve.tensor_scalar(mean[:], ps_s[:, 0, 0:D], 1.0 / NODES, None, ALU.mult)
            dve.drain()
            for t in range(TILES):
                dve.tensor_tensor(out[:, t, :], out[:, t, :], mean[:], ALU.subtract)
            dve.drain()
            for t in range(TILES):
                if t >= 2:
                    dve.wait_ge(square_summed, t - 1)
                dve.tensor_tensor(square[:, t % 2, :], out[:, t, :], out[:, t, :], ALU.mult).then_inc(square_ready, 1)
            dve.wait_ge(square_summed, TILES)
            dve.tensor_scalar(var[:], ps_s[:, 1, 0:D], 1.0 / NODES, 1e-5, ALU.mult, ALU.add)
            dve.drain()
            dve.sem_inc(root_asked, 1)
            dve.wait_ge(rooted, 1)
            dve.reciprocal(var[:], var[:])
            dve.drain()
            dve.tensor_tensor(vec[:, 1, :], vec[:, 1, :], var[:], ALU.mult)
            dve.drain()
            for t in range(TILES):
                dve.tensor_tensor(out[:, t, :], out[:, t, :], vec[:, 1, :], ALU.mult)
            dve.drain()
            for t in range(TILES):
                dve.tensor_tensor(out[:, t, :], out[:, t, :], vec[:, 2, :], ALU.add)
            dve.drain()
            for t in range(TILES):
                dve.scalar_tensor_tensor(b.x[:, t, :], out[:, t, :], 0.0, b.x[:, t, :], ALU.max, ALU.add)


def add_normalized(nc, b, node_side):
    with Phase(nc) as ctx:
        h = ctx.enter_context(nc.sbuf_tensor("back_h", [P, TILES, D], F32))
        loaded = ctx.semaphore("back_loaded")
        block = ctx.enter_context(nc.Block())

        @block.sync
        def _(sp):
            sp.dma_start(h[:], node_side[:, D:2 * D].rearrange("(t p) d -> p t d", p=P)).then_inc(loaded, 16)

        @block.vector
        def _(dve):
            dve.wait_ge(loaded, 16)
            dve.tensor_tensor(b.x[:], b.x[:], h[:], ALU.add)


def slice_attention(nc, b, h, v):
    HEADS, G, C = 8, 64, 64
    PAIR = HEADS // 2
    INNER = HEADS * C
    with Phase(nc) as ctx:
        def sb(nm, shape, dt=F32):
            return ctx.enter_context(nc.sbuf_tensor(f"sl_{nm}", shape, dt))

        def sem(nm):
            return ctx.semaphore(f"sl_{nm}")

        w_x = sb("w_x", [P, KD, INNER])
        w_x_t = sb("w_x_t", [P, PAIR, D])
        slice_w = sb("slice_w", [P, P])
        w_c = sb("w_c", [P, KD, INNER])
        bias_rows = sb("bias_rows", [PAIR, P])
        bias_cols = sb("bias_cols", [P, PAIR])
        bias_wide = sb("bias_wide", [P, PAIR, P])
        bias_c = sb("bias_c", [P, INNER])
        slice_b = sb("slice_b", [P, G])
        temp = sb("temp", [P, HEADS])
        b_out = sb("b_out", [P, D])
        logit = sb("logit", [P, 2, HEADS, G])
        soft = sb("soft", [P, 2, HEADS, G])
        small = sb("small", [P, 2, 3, HEADS])
        soft_t = sb("soft_t", [P, PAIR, ROWS])
        tok = sb("tok", [P, PAIR, D + 1])
        w_fx = sb("w_fx", [P, KD, INNER])
        b_fx = sb("b_fx", [P, INNER])
        norm = sb("norm", [P, PAIR])
        token = sb("token", [P, PAIR, C])
        token_t = sb("token_t", [C, PAIR, P])
        w_qkv = sb("w_qkv", [C, 3, C])
        asmall = sb("asmall", [G, 3, HEADS])
        w_out = sb("w_out", [C, HEADS, D])
        spare = b.xnT[:].rearrange("p k n -> p (k n)")
        tok_t = spare[:, 0:1024].rearrange("p (k a n) -> p k a n", k=KD, a=PAIR)
        q_t = spare[0:C, 1024:1536]
        k_t = spare[0:C, 1536:2048]
        val = spare[0:G, 2048:2560].rearrange("p (h c) -> p h c", h=HEADS)
        attn = spare[0:G, 2560:3072].rearrange("p (h c) -> p h c", h=HEADS)
        attn_t = spare[0:G, 3072:3584].rearrange("p (h c) -> p h c", h=HEADS)
        mixed = spare[0:C, 3584:4608].rearrange("p (h c) -> p h c", h=HEADS)
        out_w = spare[:, 4608:5632].rearrange("p (a n) -> p a n", a=PAIR)
        ps_a = ctx.enter_context(nc.psum_tensor("sl_ps_a", [P, 2, 512], F32))
        ps_t = ctx.enter_context(nc.psum_tensor("sl_ps_t", [P, 2, 512], F32))
        ps_k = ctx.enter_context(nc.psum_tensor("sl_ps_k", [P, PAIR, 512], F32))
        loaded = sem("loaded")
        slice_cleared = sem("slice_cleared")
        w_turned = sem("w_turned")
        w_kept = sem("w_kept")
        temp_ready = sem("temp_ready")
        folded = sem("folded")
        fold_kept = sem("fold_kept")
        logit_summed = sem("logit_summed")
        logit_ready = sem("logit_ready")
        exp_ready = sem("exp_ready")
        soft_ready = sem("soft_ready")
        soft_turned = sem("soft_turned")
        soft_kept = sem("soft_kept")
        tok_summed = sem("tok_summed")
        s_pe = sem("s_pe")
        s_dve = sem("s_dve")
        out_summed = sem("out_summed")
        out_kept = sem("out_kept")
        block = ctx.enter_context(nc.Block())
        LOADS = 14

        def real(t):
            return LAST if t == TILES - 1 else P

        @block.sync
        def _(sp):
            sp.dma_start(w_x[:], v["W_x"].rearrange("(k p) n -> p k n", p=P)).then_inc(loaded, 16)
            sp.wait_ge(slice_cleared, 1)
            sp.dma_start(slice_w[0:C, 0:G], v["W_slice"]).then_inc(loaded, 16)
            sp.dma_start(slice_w[C:P, G:P], v["W_slice"]).then_inc(loaded, 16)
            sp.dma_start(bias_rows[:], v["b_x"].rearrange("(a p) -> a p", p=P)).then_inc(loaded, 16)
            sp.dma_start(slice_b[:], v["b_slice"].partition_broadcast(P)).then_inc(loaded, 16)
            sp.dma_start(temp[:], v["temperature"].partition_broadcast(P)).then_inc(loaded, 16)
            sp.dma_start(b_out[:], v["b_out"].partition_broadcast(P)).then_inc(loaded, 16)
            sp.dma_start(w_fx[:], v["W_fx"].rearrange("(k p) n -> p k n", p=P)).then_inc(loaded, 16)
            sp.dma_start(b_fx[:], v["b_fx"].partition_broadcast(P)).then_inc(loaded, 16)
            for i, m in enumerate(("W_q", "W_k", "W_v")):
                sp.dma_start(w_qkv[:, i, :], v[m]).then_inc(loaded, 16)
            sp.dma_start(w_out[:, 0:4, :], v["W_out"][0:4 * C, :].rearrange("(h c) n -> c h n", c=C)).then_inc(loaded, 16)
            sp.dma_start(w_out[:, 4:8, :], v["W_out"][4 * C:8 * C, :].rearrange("(h c) n -> c h n", c=C)).then_inc(loaded, 16)

        @block.tensor
        def _(pe):
            pe.wait_ge(loaded, 16 * LOADS)
            for k in range(KD):
                for a in range(PAIR):
                    mm = pe.transpose(ps_t[:, k, a * P:(a + 1) * P], w_x[:, k, a * P:(a + 1) * P], b.ident[:])
            mm = pe.transpose(ps_k[:, 0, 0:PAIR], bias_rows[:], b.ident[0:PAIR, 0:PAIR])
            mm.then_inc(w_turned, 1)
            pe.wait_ge(w_kept, 1)
            for k in range(KD):
                for a in range(PAIR):
                    pe.matmul(ps_a[:, k, a * P:(a + 1) * P], w_x_t[:, a, k * P:(k + 1) * P], slice_w[:],
                              start=True, stop=True)
            for a in range(PAIR):
                mm = pe.matmul(ps_k[:, 1, a * P:(a + 1) * P], bias_wide[:, a, :], slice_w[:], start=True, stop=True)
            mm.then_inc(folded, 1)
            pe.wait_ge(fold_kept, 1)

            def logits(t):
                if t >= 2:
                    pe.wait_ge(logit_ready, t - 1)
                for k in range(KD):
                    mm = pe.matmul(ps_a[:, t % 2, :], b.xnT[:, k, t * P:(t + 1) * P], w_c[:, k, :],
                                   start=(k == 0), stop=(k == KD - 1))
                mm.then_inc(logit_summed, 1)

            def gather_tokens(t):
                pe.wait_ge(soft_ready, t + 1)
                if t >= 2:
                    pe.wait_ge(soft_kept, t - 1)
                for a in range(PAIR):
                    pair = soft[:, t % 2, 2 * a:2 * a + 2, :].rearrange("p h g -> p (h g)")
                    mm = pe.transpose(ps_t[:, t % 2, a * P:(a + 1) * P], pair, b.ident[:])
                mm.then_inc(soft_turned, 1)
                for a in range(PAIR):
                    pair = soft[0:real(t), t % 2, 2 * a:2 * a + 2, :].rearrange("p h g -> p (h g)")
                    mm = pe.matmul(ps_k[:, a, 0:D + 1], pair, h[0:real(t), t, :],
                                   start=(t == 0), stop=(t == TILES - 1))
                mm.then_inc(tok_summed, 1)

            for t in range(TILES):
                logits(t)
                if t:
                    gather_tokens(t - 1)
            gather_tokens(TILES - 1)

            pe.wait_ge(s_dve, 1)
            pe.wait_ge(soft_kept, TILES)
            for k in range(KD):
                for a in range(PAIR):
                    mm = pe.transpose(ps_t[:, k, a * P:(a + 1) * P], tok[:, a, k * P:(k + 1) * P], b.ident[:])
            mm.then_inc(s_pe, 1)
            pe.wait_ge(s_dve, 2)
            for a in range(PAIR):
                for k in range(KD):
                    mm = pe.matmul(ps_a[:, 0, a * P:(a + 1) * P], tok_t[:, k, a, :], w_fx[:, k, a * P:(a + 1) * P],
                                   start=(k == 0), stop=(k == KD - 1))
            mm.then_inc(s_pe, 1)
            pe.wait_ge(s_dve, 3)
            for a in range(PAIR):
                mm = pe.transpose(ps_t[0:C, 0, a * P:(a + 1) * P], token[:, a, :], b.ident[:])
            mm.then_inc(s_pe, 1)
            pe.wait_ge(s_dve, 4)
            tokens = token_t[:].rearrange("c a p -> c (a p)")
            pe.matmul(ps_k[0:C, 0, :], w_qkv[:, 0, :], tokens, start=True, stop=True)
            pe.matmul(ps_k[0:C, 1, :], w_qkv[:, 1, :], tokens, start=True, stop=True)
            for n in range(HEADS):
                mm = pe.matmul(ps_k[0:G, 2, n * C:(n + 1) * C], tokens[:, n * G:(n + 1) * G], w_qkv[:, 2, :],
                               start=True, stop=True)
            mm.then_inc(s_pe, 1)
            pe.wait_ge(s_dve, 5)
            for n in range(HEADS):
                mm = pe.matmul(ps_a[0:G, 0, n * G:(n + 1) * G], q_t[:, n * G:(n + 1) * G],
                               k_t[:, n * G:(n + 1) * G], start=True, stop=True)
            mm.then_inc(s_pe, 1)
            pe.wait_ge(s_dve, 6)
            for n in range(HEADS):
                mm = pe.transpose(ps_t[0:G, 1, n * G:(n + 1) * G], attn[:, n, :], b.ident[0:G, 0:G])
            mm.then_inc(s_pe, 1)
            pe.wait_ge(s_dve, 7)
            for n in range(HEADS):
                mm = pe.matmul(ps_a[0:C, 1, n * G:(n + 1) * G], val[:, n, :], attn_t[:, n, :], start=True, stop=True)
            mm.then_inc(s_pe, 1)
            pe.wait_ge(s_dve, 8)
            for a in range(PAIR):
                for half in range(2):
                    mm = pe.matmul(ps_k[:, a, 0:D], mixed[:, 2 * a + half, :], w_out[:, 2 * a + half, :],
                                   start=(half == 0), stop=(half == 1))
            mm.then_inc(s_pe, 1)
            pe.wait_ge(s_dve, 9)
            for t in range(TILES):
                if t >= 2:
                    pe.wait_ge(out_kept, t - 1)
                for a in range(PAIR):
                    mm = pe.matmul(ps_a[:, t % 2, 0:D], soft_t[:, a, t * P:(t + 1) * P], out_w[:, a, :],
                                   start=(a == 0), stop=(a == PAIR - 1))
                mm.then_inc(out_summed, 1)

        @block.scalar
        def _(act):
            def keep_turned(t):
                act.wait_ge(soft_turned, t + 1)
                act.activation(soft_t[:, :, t * P:(t + 1) * P], ps_t[:, t % 2, :].rearrange("p (a n) -> p a n", n=P),
                               ACT.Identity).then_inc(soft_kept, 1)

            for t in range(TILES):
                act.wait_ge(logit_ready, t + 1)
                act.activation(soft[:, t % 2, :, :], logit[:, t % 2, :, :], ACT.Exp).then_inc(exp_ready, 1)
                if t:
                    keep_turned(t - 1)
            keep_turned(TILES - 1)
            act.wait_ge(logit_ready, TILES + 1)
            act.activation(attn[:], attn[:], ACT.Exp, scale=float(C) ** -0.5).then_inc(exp_ready, 1)

        @block.vector
        def _(dve):
            dve.memset(slice_w[:], 0.0)
            dve.drain()
            dve.sem_inc(slice_cleared, 1)
            dve.wait_ge(loaded, 16 * LOADS)
            dve.tensor_scalar(temp[:], temp[:], 0.1, 5.0, ALU.max, ALU.min)
            dve.drain()
            dve.reciprocal(temp[:], temp[:])
            dve.wait_ge(w_turned, 1)
            for k in range(KD):
                dve.tensor_copy(w_x_t[:, :, k * P:(k + 1) * P], ps_t[:, k, :].rearrange("p (a n) -> p a n", n=P))
            dve.tensor_copy(bias_cols[:], ps_k[:, 0, 0:PAIR])
            dve.drain()
            dve.tensor_copy(bias_wide[:], bias_cols[:].unsqueeze(2).to_broadcast([P, PAIR, P]))
            dve.drain()
            dve.sem_inc(w_kept, 1)
            dve.wait_ge(folded, 1)

            def per_head(a):
                return a.rearrange("p (h g) -> p h g", g=G)

            inv_temp = temp[:].unsqueeze(2).to_broadcast([P, HEADS, G])
            for k in range(KD):
                dve.tensor_tensor(per_head(w_c[:, k, :]), per_head(ps_a[:, k, :]), inv_temp, ALU.mult)
            dve.tensor_tensor(per_head(bias_c[:]), per_head(ps_k[:, 1, :]),
                              slice_b[:].unsqueeze(1).to_broadcast([P, HEADS, G]), ALU.add)
            dve.drain()
            dve.tensor_tensor(per_head(bias_c[:]), per_head(bias_c[:]), inv_temp, ALU.mult)
            dve.drain()
            dve.sem_inc(fold_kept, 1)

            def center(t):
                u = t % 2
                dve.wait_ge(logit_summed, t + 1)
                dve.tensor_tensor(logit[:, u, :, :], per_head(ps_a[:, u, :]), per_head(bias_c[:]), ALU.add)
                dve.drain()
                dve.tensor_reduce(small[:, u, 0, :], logit[:, u, :, :], AX, ALU.max)
                dve.drain()
                if t >= 2:
                    dve.wait_ge(tok_summed, t - 1)
                dve.tensor_tensor(logit[:, u, :, :], logit[:, u, :, :],
                                  small[:, u, 0, :].unsqueeze(2).to_broadcast([P, HEADS, G]),
                                  ALU.subtract).then_inc(logit_ready, 1)

            def divide(t):
                u = t % 2
                dve.wait_ge(exp_ready, t + 1)
                dve.tensor_reduce(small[:, u, 1, :], soft[:, u, :, :], AX, ALU.add)
                dve.drain()
                dve.reciprocal(small[:, u, 2, :], small[:, u, 1, :])
                dve.drain()
                dve.tensor_tensor(soft[:, u, :, :], soft[:, u, :, :],
                                  small[:, u, 2, :].unsqueeze(2).to_broadcast([P, HEADS, G]),
                                  ALU.mult).then_inc(soft_ready, 1)

            for t in range(TILES):
                center(t)
                if t:
                    divide(t - 1)
            divide(TILES - 1)

            dve.wait_ge(tok_summed, TILES)
            dve.memset(mixed[:], 0.0)
            dve.tensor_copy(tok[:], ps_k[:, :, 0:D + 1])
            dve.drain()
            dve.sem_inc(s_dve, 1)
            dve.tensor_scalar(norm[:], tok[:, :, D], 1e-5, None, ALU.add)
            dve.wait_ge(s_pe, 1)
            dve.tensor_copy(tok_t[:].rearrange("p k a n -> p k (a n)"), ps_t[:])
            dve.drain()
            dve.sem_inc(s_dve, 1)
            dve.reciprocal(norm[:], norm[:])
            dve.wait_ge(s_pe, 2)
            for a in range(PAIR):
                for half in range(2):
                    rows = slice(half * G, half * G + G)
                    cols = slice(a * P + half * C, a * P + half * C + C)
                    dve.scalar_tensor_tensor(token[rows, a, :], b_fx[rows, cols], tok[rows, a, D:D + 1],
                                             ps_a[rows, 0, cols], ALU.mult, ALU.add)
            dve.drain()
            dve.tensor_tensor(token[:], token[:], norm[:].unsqueeze(2).to_broadcast([P, PAIR, C]), ALU.mult)
            dve.drain()
            dve.sem_inc(s_dve, 1)
            dve.wait_ge(s_pe, 3)
            dve.tensor_copy(token_t[:].rearrange("c a p -> c (a p)"), ps_t[0:C, 0, :])
            dve.drain()
            dve.sem_inc(s_dve, 1)
            dve.wait_ge(s_pe, 4)
            dve.tensor_copy(q_t[:], ps_k[0:C, 0, :])
            dve.tensor_copy(k_t[:], ps_k[0:C, 1, :])
            dve.tensor_copy(val[:].rearrange("g h c -> g (h c)"), ps_k[0:G, 2, :])
            dve.drain()
            dve.sem_inc(s_dve, 1)
            dve.wait_ge(s_pe, 5)
            scores = ps_a[0:G, 0, :].rearrange("p (h g) -> p h g", g=G)
            dve.tensor_reduce(asmall[:, 0, :], scores, AX, ALU.max)
            dve.drain()
            dve.tensor_tensor(attn[:], scores, asmall[:, 0, :].unsqueeze(2).to_broadcast([G, HEADS, G]),
                              ALU.subtract).then_inc(logit_ready, 1)
            dve.wait_ge(exp_ready, TILES + 1)
            dve.tensor_reduce(asmall[:, 1, :], attn[:], AX, ALU.add)
            dve.drain()
            dve.reciprocal(asmall[:, 2, :], asmall[:, 1, :])
            dve.drain()
            dve.tensor_tensor(attn[:], attn[:], asmall[:, 2, :].unsqueeze(2).to_broadcast([G, HEADS, G]), ALU.mult)
            dve.drain()
            dve.sem_inc(s_dve, 1)
            dve.wait_ge(s_pe, 6)
            dve.tensor_copy(attn_t[:].rearrange("g h k -> g (h k)"), ps_t[0:G, 1, :])
            dve.drain()
            dve.sem_inc(s_dve, 1)
            dve.wait_ge(s_pe, 7)
            for n in range(HEADS):
                half = n % 2
                dve.tensor_copy(mixed[:, n, half * G:half * G + G], ps_a[0:C, 1, n * G:(n + 1) * G])
            dve.drain()
            dve.sem_inc(s_dve, 1)
            dve.wait_ge(s_pe, 8)
            dve.tensor_copy(out_w[:], ps_k[:, :, 0:D])
            dve.drain()
            dve.sem_inc(s_dve, 1)
            for t in range(TILES):
                dve.tensor_tensor(b.x[:, t, :], b.x[:, t, :], b_out[:], ALU.add)
            dve.drain()
            for t in range(TILES):
                dve.wait_ge(out_summed, t + 1)
                dve.tensor_tensor(b.x[:, t, :], b.x[:, t, :], ps_a[:, t % 2, 0:D], ALU.add).then_inc(out_kept, 1)


def graph_ffn_stack(nc, t, out):
    def flat(name):
        a = t[name]
        if len(a.shape) == 1:
            return a
        dims = " ".join(f"d{i}" for i in range(len(a.shape)))
        return a.rearrange(f"{dims} -> ({dims})")

    with ExitStack() as ctx:
        b = persistent(nc, ctx)
        prepare(nc, b, t["x"], t["src"], t["dst"], flat("edge_attr3_1x1"), flat("edge_attr_2"), t["edge_weight"])

        with ExitStack() as layer:
            acc = layer.enter_context(nc.sbuf_tensor("g0_acc", [P, TILES, 4, 65], F32))
            best = layer.enter_context(nc.sbuf_tensor("g0_best", [P, TILES, 4], F32))
            part = layer.enter_context(nc.sbuf_tensor("g0_part", [P, TILES, 4], F32))
            normalize(nc, b, "n0")
            attention_tables(nc, b, "t0", t["L0_gnn_W"], flat("L0_gnn_w_att_src"), flat("L0_gnn_w_att_dst"),
                             4, b.table["att0"], acc, best, part, False)
            attend(nc, b, "g0", 4, b.table["att0"], acc, best, part, use_dist=True)
            close_first(nc, b, acc)

        with ExitStack() as layer:
            y = layer.enter_context(nc.sbuf_tensor("f0_y", [P, TILES, D], F32))
            gates = layer.enter_context(nc.sbuf_tensor("f0_gates", [P, TILES, 16], F32))
            shift = layer.enter_context(nc.sbuf_tensor("f0_shift", [P, 64], F32))
            normalize(nc, b, "n1", y)
            route(nc, b, "r0", 16, "top2", t["L0_ffn_gate_w"], t["L0_ffn_gate_b"], t["L0_ffn_b2"], y, y, gates,
                  [(shift[:], "copy", [t["L0_ffn_b1"].rearrange("e (f p) -> (e f) p", p=P)])])
            run_experts(nc, b, "f0", 16, [t["L0_ffn_w1"], t["L0_ffn_w2"]], [(None, shift)], gates, y)
            close_moe(nc, b, y, t["L0_ffn_gamma"], t["L0_ffn_beta"])

        with ExitStack() as layer:
            h = layer.enter_context(nc.sbuf_tensor("g1_h", [P, TILES, D], F32))
            normalize(nc, b, "n2", h)
            for n, heads in ((1, 4), (2, 1)):
                with ExitStack() as conv:
                    acc = conv.enter_context(nc.sbuf_tensor(f"g{n}_acc", [P, TILES, heads, D // heads + 1], F32))
                    best = conv.enter_context(nc.sbuf_tensor(f"g{n}_best", [P, TILES, heads], F32))
                    part = conv.enter_context(nc.sbuf_tensor(f"g{n}_part", [P, TILES, heads], F32))
                    attention_tables(nc, b, f"t{n}", t[f"L1_gnn_W{n}"], flat(f"L1_gnn_att_src{n}"),
                                     flat(f"L1_gnn_att_dst{n}"), heads, b.table[f"att{n}"], acc, best, part, True)
                    attend(nc, b, f"g{n}", heads, b.table[f"att{n}"], acc, best, part)
                    over_denominators(nc, b, f"o{n}", acc, h, t[f"L1_gnn_bias{n}"], 1e-16, True)
                if n == 1:
                    turn_tiles(nc, b, "turn1", h)
            close_gat(nc, b, h, [t[f"L1_gnn_{v}"] for v in
                                 ("bn_gamma", "bn_beta", "bn_mean", "bn_var", "ln_gamma", "ln_beta")])

        with ExitStack() as layer:
            gates = layer.enter_context(nc.sbuf_tensor("f1_gates", [P, TILES, 8], F32))
            cols = layer.enter_context(nc.sbuf_tensor("f1_cols", [P, 2, 2, 16], F32))
            normalize(nc, b, "n3")

            def rows(name):
                return t[f"L1_ffn_{name}"].rearrange("e (f p) -> (e f) p", p=P)

            route(nc, b, "r1", 8, "all", t["L1_ffn_Wr"], t["L1_ffn_br"], t["L1_ffn_bo"], b.x, b.x, gates,
                  [([cols[:, i, 0, :], cols[:, i, 1, :]], "norm",
                    [rows(f"{v}{i + 1}") for v in ("g", "be", "m", "v", "b")]) for i in range(2)])
            run_experts(nc, b, "f1", 8, [t["L1_ffn_W1"], t["L1_ffn_W2"], t["L1_ffn_Wo"]],
                        [(cols[:, i, 0, :], cols[:, i, 1, :]) for i in range(2)], gates, b.x)

        node_side = nc.dram_tensor("node_side", (ROWS, 2 * D), F32, kind="Internal").ap()
        with ExitStack() as layer:
            edge_abs = layer.enter_context(nc.sbuf_tensor("edge_abs", [P, SLOTS, SUB], F32))
            with ExitStack() as first:
                h = first.enter_context(nc.sbuf_tensor("g2_h", [P, TILES, D], F32))
                normalize(nc, b, "n4", h)
                direction_tables(nc, b, "t2b", h, t["L2_gnn_W1"], t["L2_gnn_b1"], b.table["dir"], node_side, edge_abs)
            acc = layer.enter_context(nc.sbuf_tensor("dir_acc", [P, TILES, 3, D + 1], F32))
            direct(nc, b, "dir", b.table["dir"], acc, edge_abs)
            close_direction(nc, b, acc, node_side, t["L2_gnn_W2"], t["L2_gnn_b2"], flat("node_vec1"),
                            t["L2_gnn_gamma"], t["L2_gnn_beta"])
        add_normalized(nc, b, node_side)

        with ExitStack() as layer:
            h = layer.enter_context(nc.sbuf_tensor("sl_h", [P, TILES, D + 1], F32))
            normalize(nc, b, "n5", h)
            slice_attention(nc, b, h, {v: flat(f"L2_ffn_{v}") if v[0] in "bt" else t[f"L2_ffn_{v}"] for v in
                                       ("W_fx", "b_fx", "W_x", "b_x", "W_slice", "b_slice", "W_q", "W_k", "W_v",
                                        "W_out", "b_out", "temperature")})

        with ExitStack() as layer:
            acc = layer.enter_context(nc.sbuf_tensor("g3_acc", [P, TILES, 8, 33], F32))
            best = layer.enter_context(nc.sbuf_tensor("g3_best", [P, TILES, 8], F32))
            part = layer.enter_context(nc.sbuf_tensor("g3_part", [P, TILES, 8], F32))
            x_r = layer.enter_context(nc.sbuf_tensor("g3_x_r", [P, TILES, D], F32))
            att = layer.enter_context(nc.sbuf_tensor("g3_att", [P, D], F32))
            normalize(nc, b, "n6")
            pair_tables(nc, b, "t3", t["L3_gnn_W_l"], t["L3_gnn_b_l"], t["L3_gnn_W_r"], t["L3_gnn_b_r"],
                        flat("L3_gnn_att"), b.table["att3"], x_r, acc, best, part, att)
            attend(nc, b, "g3", 8, b.table["att3"], acc, best, part, pair_dots=(x_r, att))
            over_denominators(nc, b, "o3", acc, x_r, t["L3_gnn_bias"], 1e-16, False)
            add_to_stream(nc, b, x_r)

        with ExitStack() as layer:
            gates = layer.enter_context(nc.sbuf_tensor("f3_gates", [P, TILES, 6], F32))
            shift = layer.enter_context(nc.sbuf_tensor("f3_shift", [P, 2, 12], F32))
            normalize(nc, b, "n7")
            route(nc, b, "r3", 6, "top2 of softmax", t["L3_ffn_router_w2"], t["L3_ffn_router_b2"],
                  t["L3_ffn_expert_b3"], b.x, b.x, gates,
                  [(shift[:, i, :], "copy", [t[f"L3_ffn_expert_b{i + 1}"].rearrange("e (f p) -> (e f) p", p=P)])
                   for i in range(2)], first=(t["L3_ffn_router_w1"], t["L3_ffn_router_b1"]))
            run_experts(nc, b, "f3", 6, [t[f"L3_ffn_expert_w{i}"] for i in (1, 2, 3)],
                        [(None, shift[:, i, :]) for i in range(2)], gates, b.x)

        store_stream(nc, b, out)


def kernel(**inputs):
    import concourse.bacc as bacc
    from concourse.bass_utils import run_bass_kernel_spmd

    nc = bacc.Bacc("TRN2", target_bir_lowering=False, num_devices=1)
    arrays, args = {}, {}
    for name, value in inputs.items():
        a = np.ascontiguousarray(value)
        arrays[f"in_{name}"] = a
        args[name] = nc.dram_tensor(f"in_{name}", a.shape, mybir.dt.from_np(a.dtype), kind="ExternalInput").ap()
    out = nc.dram_tensor("out_stream", (NODES, D), F32, kind="ExternalOutput").ap()
    graph_ffn_stack(nc, args, out)
    result = run_bass_kernel_spmd(nc, [arrays], core_ids=[0])
    return result.results[0]["out_stream"]
```
